# Optimizing a Trainium2 kernel written in Bass

```python
import numpy as np
import jax
import jax.numpy as jnp

def _softmax(x, axis=-1):
    return jax.nn.softmax(x, axis=axis)

def _gelu(x):
    return jax.nn.gelu(x, approximate=True)

def _silu(x):
    return jax.nn.silu(x)

def _sigmoid(x):
    return jax.nn.sigmoid(x)

def _layernorm(x, axis=-1, eps=1e-05):
    m = jnp.mean(x, axis=axis, keepdims=True)
    v = jnp.var(x, axis=axis, keepdims=True)
    return (x - m) / jnp.sqrt(v + eps)

def _scatter_add(tgt, idx, src, axis=0):
    return tgt.at[idx].add(src)

def _segment_sum(src, seg, n):
    return jax.ops.segment_sum(src, seg, n)
kernel_name = 'mk_vit_tower_d1_tok_img1024_r4_8557c3'

def setup_inputs(seed: int=0):
    np.random.seed(seed)
    _w = jnp.asarray

    def _rec_inputs():
        import jax
        import jax.numpy as jnp
        _rk = jax.random.key(seed)
        x = -0.000222058 + 0.999998 * jax.random.normal(jax.random.fold_in(_rk, 1), (64, 3, 64, 64), jnp.float32)
        return x
    x = _rec_inputs()

    def _L0_tok_setup():
        import jax, jax.numpy as jnp
        import numpy as np
        IMG, PS, C, OUT = (64, 16, 3, 256)
        NP = IMG // PS
        IN_FEAT = C * PS * PS
        key = jax.random.key(seed)
        k1, k2, k3, k4 = jax.random.split(key, 4)
        x = jax.random.normal(k1, (128, C, IMG, IMG), dtype=jnp.float32)
        W = jax.random.normal(k2, (OUT, IN_FEAT), dtype=jnp.float32) / np.sqrt(IN_FEAT)
        b = jax.random.normal(k3, (OUT,), dtype=jnp.float32) * 0.01
        pos_emb = jax.random.normal(k4, (NP * NP, OUT), dtype=jnp.float32)
        return {'x': x, 'W': W, 'b': b, 'pos_emb': pos_emb}
    _L0_tok_all = _L0_tok_setup()
    _L0_tok_in = {k: v for k, v in _L0_tok_all.items() if k in ('W', 'b', 'pos_emb')}
    del _L0_tok_all

    def _L0_attn_setup():
        import jax, jax.numpy as jnp
        import numpy as np
        N_HEADS = 16
        LN_EPS = 1e-05

        def _rope_tables(T, d_head, dtype):
            i = jnp.arange(1, d_head // 2 + 1, dtype=dtype)
            thetas = jnp.repeat(1000.0 ** (-2.0 * i / d_head), 2)
            pos = jnp.arange(1, T + 1, dtype=dtype)
            args = pos[:, None] * thetas[None, :]
            return (jnp.sin(args), jnp.cos(args))

        def _apply_rope(x, sin, cos):
            x_odd = x[..., ::2]
            x_even = x[..., 1::2]
            x_sin = jnp.stack([-x_even, x_odd], axis=-1).reshape(x.shape)
            return x * cos + x_sin * sin
        key = jax.random.key(seed)
        k1, k2, k3 = jax.random.split(key, 3)
        B, T, C = (2, 512, 256)
        x = jax.random.normal(k1, (B, T, C), dtype=jnp.float32)
        w_in = jax.random.normal(k2, (3 * C, C), dtype=jnp.float32) * 0.02
        w_out = jax.random.normal(k3, (C, C), dtype=jnp.float32) * 0.02
        ln_gamma = jnp.ones((C,), dtype=jnp.float32)
        ln_beta = jnp.zeros((C,), dtype=jnp.float32)
        return {'x': x, 'w_in': w_in, 'w_out': w_out, 'ln_gamma': ln_gamma, 'ln_beta': ln_beta}
    _L0_attn_all = _L0_attn_setup()
    _L0_attn_in = {k: v for k, v in _L0_attn_all.items() if k in ('w_in', 'w_out', 'ln_gamma', 'ln_beta')}
    del _L0_attn_all

    def _L0_ffn_setup():
        import jax, jax.numpy as jnp
        import numpy as np
        SWIGLU_ALPHA = 1.702
        SWIGLU_LIMIT = 7.0
        TOP_K = 4
        key = jax.random.key(seed)
        k = jax.random.split(key, 5)
        B, S, D, E, I = (2, 256, 256, 8, 512)
        return {'hidden_states': jax.random.normal(k[0], (B, S, D), dtype=jnp.float32), 'router_weight': jax.random.normal(k[1], (E, D), dtype=jnp.float32) * 0.02, 'router_bias': jnp.zeros((E,), dtype=jnp.float32), 'gate_up_proj': jax.random.normal(k[2], (E, 2 * I, D), dtype=jnp.float32) * 0.02, 'gate_up_proj_bias': jnp.zeros((E, 2 * I), dtype=jnp.float32), 'down_proj': jax.random.normal(k[3], (E, D, I), dtype=jnp.float32) * 0.02, 'down_proj_bias': jnp.zeros((E, D), dtype=jnp.float32)}
    _L0_ffn_all = _L0_ffn_setup()
    _L0_ffn_in = {k: v for k, v in _L0_ffn_all.items() if k in ('router_weight', 'router_bias', 'gate_up_proj', 'gate_up_proj_bias', 'down_proj', 'down_proj_bias')}
    del _L0_ffn_all
    return {'x': x, 'L0_tok_W': _L0_tok_in['W'], 'L0_tok_b': _L0_tok_in['b'], 'L0_tok_pos_emb': _L0_tok_in['pos_emb'], 'L0_attn_w_in': _L0_attn_in['w_in'], 'L0_attn_w_out': _L0_attn_in['w_out'], 'L0_attn_ln_gamma': _L0_attn_in['ln_gamma'], 'L0_attn_ln_beta': _L0_attn_in['ln_beta'], 'L0_ffn_router_weight': _L0_ffn_in['router_weight'], 'L0_ffn_router_bias': _L0_ffn_in['router_bias'], 'L0_ffn_gate_up_proj': _L0_ffn_in['gate_up_proj'], 'L0_ffn_gate_up_proj_bias': _L0_ffn_in['gate_up_proj_bias'], 'L0_ffn_down_proj': _L0_ffn_in['down_proj'], 'L0_ffn_down_proj_bias': _L0_ffn_in['down_proj_bias']}

def reference(x, L0_tok_W, L0_tok_b, L0_tok_pos_emb, L0_attn_w_in, L0_attn_w_out, L0_attn_ln_gamma, L0_attn_ln_beta, L0_ffn_router_weight, L0_ffn_router_bias, L0_ffn_gate_up_proj, L0_ffn_gate_up_proj_bias, L0_ffn_down_proj, L0_ffn_down_proj_bias):
    import jax
    import jax.numpy as jnp

    def _L0_tok_ref(x, W, b, pos_emb):
        import jax, jax.numpy as jnp
        import numpy as np
        IMG, PS, C, OUT = (64, 16, 3, 256)
        NP = IMG // PS
        IN_FEAT = C * PS * PS
        B = x.shape[0]
        p = x.reshape(B, C, NP, PS, NP, PS).transpose(0, 1, 2, 4, 3, 5)
        p = p.transpose(0, 2, 3, 1, 4, 5)
        p = p.reshape(B, NP * NP, IN_FEAT)
        out = jnp.einsum('bnf,of->bno', p, W) + b + pos_emb
        return out

    def _L0_attn_ref(x, w_in, w_out, ln_gamma, ln_beta):
        import jax, jax.numpy as jnp
        import numpy as np
        N_HEADS = 16
        LN_EPS = 1e-05

        def _rope_tables(T, d_head, dtype):
            i = jnp.arange(1, d_head // 2 + 1, dtype=dtype)
            thetas = jnp.repeat(1000.0 ** (-2.0 * i / d_head), 2)
            pos = jnp.arange(1, T + 1, dtype=dtype)
            args = pos[:, None] * thetas[None, :]
            return (jnp.sin(args), jnp.cos(args))

        def _apply_rope(x, sin, cos):
            x_odd = x[..., ::2]
            x_even = x[..., 1::2]
            x_sin = jnp.stack([-x_even, x_odd], axis=-1).reshape(x.shape)
            return x * cos + x_sin * sin
        B, T, C = x.shape
        H = N_HEADS
        d_head = C // H
        scale = 1.0 / jnp.sqrt(jnp.asarray(d_head, dtype=x.dtype))
        qkv = jnp.einsum('btc,oc->bto', x, w_in)
        q, k, v = jnp.split(qkv, 3, axis=-1)
        q = q.reshape(B, T, H, d_head).transpose(0, 2, 1, 3)
        k = k.reshape(B, T, H, d_head).transpose(0, 2, 1, 3)
        v = v.reshape(B, T, H, d_head).transpose(0, 2, 1, 3)
        sin, cos = _rope_tables(T, d_head, x.dtype)
        q_rope = _apply_rope(q, sin, cos)
        k_rope = _apply_rope(k, sin, cos)
        att_num = jnp.exp(jnp.einsum('bhqd,bhkd->bhqk', q_rope, k_rope) * scale)
        att_den = jnp.sum(jnp.exp(jnp.einsum('bhqd,bhkd->bhqk', q, k) * scale), axis=-1, keepdims=True)
        att = att_num / att_den
        y = jnp.einsum('bhqk,bhkd->bhqd', att, v)
        y = y.transpose(0, 2, 1, 3).reshape(B, T, C)
        y = jnp.einsum('btc,oc->bto', y, w_out)
        h = y + x
        mu = jnp.mean(h, axis=-1, keepdims=True)
        var = jnp.var(h, axis=-1, keepdims=True)
        return (h - mu) / jnp.sqrt(var + LN_EPS) * ln_gamma + ln_beta

    def _L0_ffn_ref(hidden_states, router_weight, router_bias, gate_up_proj, gate_up_proj_bias, down_proj, down_proj_bias):
        import jax, jax.numpy as jnp
        import numpy as np
        SWIGLU_ALPHA = 1.702
        SWIGLU_LIMIT = 7.0
        TOP_K = 4
        B, S, D = hidden_states.shape
        E = router_weight.shape[0]
        x = hidden_states.reshape(-1, D)
        N = x.shape[0]
        logits = x @ router_weight.T + router_bias
        topk_logits, topk_idx = jax.lax.top_k(logits, TOP_K)
        topk_w = jax.nn.softmax(topk_logits.astype(jnp.float32), axis=-1)
        combine = jnp.zeros((N, E), dtype=jnp.float32)
        combine = combine.at[jnp.arange(N)[:, None], topk_idx].set(topk_w)
        gate_up = jnp.einsum('nd,ejd->nej', x, gate_up_proj) + gate_up_proj_bias
        gate, up = jnp.split(gate_up, 2, axis=-1)
        gate = jnp.minimum(gate, SWIGLU_LIMIT)
        up = jnp.clip(up, -SWIGLU_LIMIT, SWIGLU_LIMIT)
        act = (up + 1.0) * gate * jax.nn.sigmoid(SWIGLU_ALPHA * gate)
        out = jnp.einsum('nei,edi->ned', act, down_proj) + down_proj_bias
        y = jnp.einsum('ned,ne->nd', out, combine.astype(out.dtype))
        return y.reshape(B, S, D)
    h = _L0_tok_ref(x, L0_tok_W, L0_tok_b, L0_tok_pos_emb)
    h = h + _L0_attn_ref(_layernorm(h, axis=-1), L0_attn_w_in, L0_attn_w_out, L0_attn_ln_gamma, L0_attn_ln_beta)
    h = h + _L0_ffn_ref(_layernorm(h, axis=-1), L0_ffn_router_weight, L0_ffn_router_bias, L0_ffn_gate_up_proj, L0_ffn_gate_up_proj_bias, L0_ffn_down_proj, L0_ffn_down_proj_bias)
    return h

_drawn_inputs = setup_inputs


def setup_inputs(seed=0):
    import zlib

    import numpy as np

    out = dict(_drawn_inputs(seed))
    spreads = {'L0_attn_ln_gamma': (1.0, 0.2),
     'L0_attn_ln_beta': (0.0, 0.1),
     'L0_ffn_router_bias': (0.0, 0.758),
     'L0_ffn_gate_up_proj_bias': (0.0, 0.8),
     'L0_ffn_down_proj_bias': (0.0, 0.399)}
    factors = {'L0_tok_b': 7.697,
     'L0_attn_w_in': 5.359,
     'L0_attn_w_out': 5.183,
     'L0_ffn_router_weight': 2.945,
     'L0_ffn_gate_up_proj': 3.302,
     'L0_ffn_down_proj': 3.138}
    for name, (base, spread) in spreads.items():
        noise = np.random.default_rng([zlib.crc32(name.encode()), seed]).standard_normal(out[name].shape)
        drawn = base * np.exp(spread * noise) if base else spread * noise
        out[name] = jnp.asarray(drawn.astype(out[name].dtype))
    for name, factor in factors.items():
        out[name] = (out[name] * factor).astype(out[name].dtype)
    return out
```

```python
from contextlib import ExitStack

import numpy as np

import concourse.bass as bass
from concourse import mybir

P = 128
ALU = mybir.AluOpType
ACT = mybir.ActivationFunctionType
AX = mybir.AxisListType.X
F32 = mybir.dt.float32
F32R = mybir.dt.float32r
BF16 = mybir.dt.bfloat16

IMAGES, CH, IMG, PS = 64, 3, 64, 16
GRID = IMG // PS
SEQ = GRID * GRID
TOK = IMAGES * SEQ
NT = TOK // P
HALF = TOK // 2
TPH = NT // 2
D = 256
DK = D // P
FEAT = CH * PS * PS
FK = FEAT // P
HEADS, DH = 16, 16
SCALE = 1.0 / 4.0
EXPERTS, INNER, TOPK = 8, 512, 4
IC = INNER // P
ALPHA, LIMIT = 1.702, 7.0
EPS = 1e-5
QKV = 5 * D
GU = DK * 2 * INNER
WCOLS = GU + IC * D
WROW = WCOLS + 2 * IC
PIECE = 512
PIECES = WCOLS // PIECE

C_ID, C_MASK, C_EVEN, C_ODD, C_COS, C_SIN, C_TRI = 0, 128, 160, 161, 162, 178, 194
C_COLS = C_TRI + EXPERTS * EXPERTS


def stages():
    def front(t):
        return [("tok", t)]

    def turn(t):
        return [("norm1", t), ("x1T", t)]

    order = front(0) + front(1) + turn(0) + front(2) + turn(1) + front(3) + turn(2) + front(4) + turn(3)
    for half in range(2):
        for c in range(DK):
            order += [("q", (half, c)), ("qs", (half, c)), ("k", (half, c)), ("ks", (half, c))]
        order += [("v", t) for t in range(half * TPH, half * TPH + TPH)]
        for i in range(TPH):
            t = half * TPH + i
            order += [("scores", t)]
            if t >= 2:
                order += [("norm3", t - 2), ("x2T", t - 2)]
            if t >= 1:
                order += [("yT", t - 1)]
            order += [("mask", t), ("mix", t)]
            if t >= 1:
                order += [("proj", t - 1), ("norm2", t - 1)]
            if t >= 2:
                order += [("logits", t - 2)]
            if half == 0:
                order += turn(TPH + i) + ([("tok", TPH + 1 + i)] if i + 1 < TPH else [])
            else:
                order += [("split", 2 * i), ("split", 2 * i + 1)] if i < PIECES // 2 else []
    t = NT - 1
    order += [("norm3", t - 1), ("x2T", t - 1), ("yT", t), ("proj", t), ("norm2", t), ("logits", t - 1),
              ("norm3", t), ("x2T", t), ("logits", t)]
    return order


RELEASES = {"tok": 1, "x1T": 1, "q": 2, "qs": 1, "k": 2, "ks": 1, "v": 1, "yT": 1, "proj": 1, "x2T": 1, "logits": 1,
            "cT": 1, "cTf": 1, "bias": 1, "share": 1, "out": 1}
RING = 4


def build(nc, A_x, A_wtok, A_tokb, A_pos, A_wqkv, A_wo, A_gamma, A_beta, A_rw, A_rb, A_wffn, A_bdown, A_const,
          A_sel, out):
    order = stages()
    jobs = [s for s in order if s[0] in RELEASES]
    jobs += [("cT", 0), ("cTf", 0), ("cTf", 1)] + [("bias", (c, h)) for h in range(2) for c in range(DK)]
    jobs += [("share", (e, h)) for e in range(EXPERTS) for h in range(2)]
    jobs += [("out", t) for t in range(NT)]
    number = {job: n for n, job in enumerate(jobs)}
    through, total = [], [0] * RING
    for n, (kind, _) in enumerate(jobs):
        total[n % RING] += RELEASES[kind]
        through.append(total[n % RING])

    with ExitStack() as ctx:
        def sb(name, shape, dt=F32):
            return ctx.enter_context(nc.sbuf_tensor(name, shape, dt))

        def sem(name):
            return ctx.enter_context(nc.semaphore(name))

        banks = [ctx.enter_context(nc.psum_tensor(f"bank{i}", [P, 512], F32)) for i in range(RING)]
        scores = ctx.enter_context(nc.psum_tensor("scores", [P, 4, 512], F32))
        gate_ps, up_ps = [scores[:, 0, :], scores[:, 1, :]], [scores[:, 2, :], scores[:, 3, :]]
        y_ps = [banks[0], banks[1]]

        const = sb("const", [P, C_COLS])
        ident = const[:, C_ID:C_ID + P]
        even, odd = const[:, C_EVEN:C_EVEN + 1], const[:, C_ODD:C_ODD + 1]
        sel = sb("sel", [P, EXPERTS, P], BF16)
        identb = sb("identb", [P, P], BF16)
        pos = sb("pos", [P, D])
        tokb = sb("tokb", [P, D])
        gamma = sb("gamma", [P, D])
        beta = sb("beta", [P, D])
        rb = sb("rb", [P, EXPERTS])
        rw = sb("rw", [P, DK, EXPERTS])
        rwh = sb("rwh", [P, DK, EXPERTS], F32R)
        rwl = sb("rwl", [P, DK, EXPERTS], F32R)
        bdown = sb("bdown", [EXPERTS, D])
        wo = sb("wo", [P, DK, D])
        raw = [sb(f"raw{i}", [P, WROW]) for i in range(2)]
        patches = raw[0][:, 0:4 * FK * P].rearrange("p (b k n) -> p b k n", b=4, k=FK)
        bias = [sb(f"bias{i}", [P, 2 * IC]) for i in range(2)]
        whi = [sb(f"whi{i}", [P, WCOLS], F32R) for i in range(2)]
        wlo = [sb(f"wlo{i}", [P, WCOLS], F32R) for i in range(2)]
        xh = sb("xh", [P, DK, TOK], F32R)
        xl = sb("xl", [P, DK, TOK], F32R)
        h = sb("h", [P, NT, D])
        x1 = sb("x1", [P, NT, D])
        yacc = sb("yacc", [P, DK, TOK])
        wtok = yacc[:, :, 0:FK * D // DK].rearrange("p c (k n) -> p c k n", n=D)
        shares = sb("shares", [P, EXPERTS * TOK])
        qn = shares[:, 0:1024].rearrange("p (c n) -> p c n", c=DK)
        kr = shares[:, 1024:2048].rearrange("p (c n) -> p c n", c=DK)
        kz = shares[:, 2048:4096].rearrange("p (c s n) -> p c s n", c=DK, s=2)
        qz = shares[:, 4096:6144].rearrange("p (c s n) -> p c s n", c=DK, s=2)
        v = shares[:, 6144:7168].rearrange("p (t n) -> p t n", t=TPH)
        yt = shares[:, 7168:7680].rearrange("p (b c n) -> p b c n", b=2, c=DK)
        x2 = shares[:, 7680:8192].rearrange("p (b n) -> p b n", b=2)
        halves = sb("halves", [P, 2 * DK * QKV], F32R)
        wqh = halves[:, 0:DK * QKV].rearrange("p (c n) -> p c n", c=DK)
        wql = halves[:, DK * QKV:2 * DK * QKV].rearrange("p (c n) -> p c n", c=DK)
        ah = halves[:, 0:2048].rearrange("p (b n) -> p b n", b=4)
        al = halves[:, 2048:4096].rearrange("p (b n) -> p b n", b=4)
        work = sb("work", [P, 10 * 512])
        wk = work[:, :].rearrange("p (s b n) -> p s b n", s=5, b=2)
        gate, tanh, up, act = wk[:, 0], wk[:, 1], wk[:, 2], wk[:, 3]
        e_sb = work[:, 0:2048].rearrange("p (b i y n) -> p b i y n", b=2, i=4, y=2)
        p_sb = work[:, 2048:3072].rearrange("p (b i n) -> p b i n", b=2, i=4)
        ropec = work[:, 3072:4096].rearrange("p (b n) -> p b n", b=2)
        ropes = work[:, 4096:5120].rearrange("p (b n) -> p b n", b=2)
        yn = sb("yn", [P, 2, D])
        z = sb("z", [P, 2, D])
        den = sb("den", [P, 2, HEADS])
        rden = sb("rden", [P, 2, HEADS])
        stat = sb("stat", [P, 3, NT, 6])
        mv = sb("mv", [P, 3, NT, 2])
        ve = sb("ve", [P, 3, NT, 1])
        rstd = sb("rstd", [P, 3, NT, 1])
        power = sb("power", [P, 1])
        offset = sb("offset", [P, 2 * IC])
        lg = sb("lg", [P, NT, EXPERTS])
        lmax = sb("lmax", [P, NT])
        ex = sb("ex", [P, NT, EXPERTS])
        pair = work[:, 0:2 * NT * EXPERTS * EXPERTS].rearrange("p (b n) -> p b n", b=2)
        rank = sb("rank", [P, NT, EXPERTS])
        comb = sb("comb", [P, NT, EXPERTS])
        rest = sb("rest", [P, NT, EXPERTS])
        parts = sb("parts", [P, NT, 3, EXPERTS], BF16)
        cT = sb("cT", [P, TOK], BF16)
        cTf = sb("cTf", [EXPERTS, TOK])
        ot = z

        wtok_in, const_in, rows_in, wqkv_in, small_in = (sem(n) for n in ("wtok_in", "const_in", "rows_in",
                                                                         "wqkv_in", "small_in"))
        patch_in = [sem(f"patch_in{i}") for i in range(4)]
        raw_in = [sem(f"raw_in{i}") for i in range(2)]
        ready = sem("ring_ready")
        free = [sem(f"ring_free{i}") for i in range(RING)]
        chain, pchain, achain = sem("dve_chain"), sem("pool_chain"), sem("act_chain")
        pos_ready, power_ready, cz_ready = sem("pos_ready"), sem("power_ready"), sem("cz_ready")
        wqh_ready, wql_ready, rw_ready = sem("wqh_ready"), sem("wql_ready"), sem("rw_ready")
        identb_ready = sem("identb_ready")
        var_ready = [sem(f"var_ready{i}") for i in range(3)]
        rstd_ready = [sem(f"rstd_ready{i}") for i in range(3)]
        x1_ready, xhi_ready, x2_ready, x2hi_ready = sem("x1_ready"), sem("xhi_ready"), sem("x2_ready"), sem("x2hi_ready")
        roped = sem("roped")
        scored, exped, p_ready, den_ready = sem("scored"), sem("exped"), sem("p_ready"), sem("den_ready")
        mixed, y_ready, zn_ready, h1_ready = sem("mixed"), sem("y_ready"), sem("zn_ready"), sem("h1_ready")
        lsub_ready, ex_ready, parts_ready = sem("lsub_ready"), sem("ex_ready"), sem("parts_ready")
        whi_ready, wlo_ready, bias_ready = sem("whi_ready"), sem("wlo_ready"), sem("bias_ready")
        gu_ready, gate_done, up_done, tanh_done = sem("gu_ready"), sem("gate_done"), sem("up_done"), sem("tanh_done")
        s_done, m_done, a_done = sem("s_done"), sem("m_done"), sem("a_done")
        ah_ready, al_ready, down_done, y_added = sem("ah_ready"), sem("al_ready"), sem("down_done"), sem("y_added")
        ot_ready, out_done = sem("ot_ready"), [sem("out_done0"), sem("out_done1")]

        def bank(job):
            return banks[number[job] % RING]

        def arrived(eng, job):
            eng.wait_ge(ready, number[job] + 1)

        def freed(job):
            return free[number[job] % RING]

        def taken(eng, job):
            eng.wait_ge(freed(job), through[number[job]])

        block = ctx.enter_context(nc.Block())

        @block.sync
        def _(sp):
            sp.dma_start(wtok, A_wtok.rearrange("p (c k) n -> p c k n", c=DK)).then_inc(wtok_in, 16)
            sp.dma_start(patches[:, 0], A_x[0]).then_inc(patch_in[0], 16)
            sp.dma_start(const[:], A_const).then_inc(const_in, 16)
            for i in range(P // SEQ):
                sp.dma_start(pos[i * SEQ:(i + 1) * SEQ, :], A_pos).then_inc(rows_in, 16)
            sp.dma_start(tokb[:], A_tokb.partition_broadcast(P)).then_inc(rows_in, 16)
            for t in range(1, 4):
                sp.dma_start(patches[:, t], A_x[t]).then_inc(patch_in[t], 16)
            sp.dma_start(raw[1][:, 0:DK * QKV], A_wqkv).then_inc(wqkv_in, 16)
            sp.dma_start(gamma[:], A_gamma.partition_broadcast(P)).then_inc(small_in, 16)
            sp.dma_start(beta[:], A_beta.partition_broadcast(P)).then_inc(small_in, 16)
            sp.dma_start(rb[:], A_rb.partition_broadcast(P)).then_inc(small_in, 16)
            sp.dma_start(rw[:], A_rw).then_inc(small_in, 16)
            sp.dma_start(wo[:], A_wo).then_inc(small_in, 16)
            sp.dma_start(bdown[:], A_bdown).then_inc(small_in, 16)
            sp.dma_start(sel[:], A_sel).then_inc(small_in, 16)
            for t in range(4, NT):
                arrived(sp, ("tok", t - 4))
                sp.dma_start(patches[:, t % 4], A_x[t]).then_inc(patch_in[t % 4], 16)
            arrived(sp, ("tok", NT - 1))
            sp.dma_start(raw[0][:], A_wffn[0]).then_inc(raw_in[0], 16)
            sp.wait_ge(wqh_ready, 1)
            sp.wait_ge(wql_ready, 1)
            sp.dma_start(raw[1][:], A_wffn[1]).then_inc(raw_in[1], 16)
            with sp.Fori(1, EXPERTS // 2) as it:
                for i in range(2):
                    sp.wait_ge(wlo_ready, it * (2 * PIECES) + (i - 1) * PIECES)
                    sp.dma_start(raw[i][:], A_wffn[bass.ds(it * 2 + i, 1)].rearrange("e p n -> (e p) n"))\
                        .then_inc(raw_in[i], 16)
            for t in range(NT):
                sp.wait_ge(ot_ready, t + 1)
                sp.dma_start(out[t * P:(t + 1) * P, :], ot[:, t % 2]).then_inc(out_done[t % 2], 16)
            sp.wait_ge(out_done[0], 16 * (NT // 2))
            sp.wait_ge(out_done[1], 16 * (NT // 2))

        def loop(eng, step, first):
            per = 2 * 2 * IC
            for p in range(first):
                step(0, p)
            with eng.Fori(0, EXPERTS // 2 - 1) as it:
                for p in range(first, first + per):
                    step(it, p)
            for p in range(first, per + 4):
                step(EXPERTS // 2 - 1, p)

        PER = 2 * 2 * IC
        STEPS = EXPERTS * 2 * IC
        LAST = EXPERTS // 2 - 1

        def beyond(it, p):
            return isinstance(it, int) and it == LAST and p >= PER

        def split_piece(p):
            k = p % (2 * IC) - 2
            return ((p // (2 * IC) + 1) % 2, k) if 0 <= k < PIECES else None

        @block.tensor
        def _(pe):
            def claim(job):
                n = number[job]
                if n >= RING:
                    pe.wait_ge(free[n % RING], through[n - RING])

            def split_product(dst, wh, wl, xhi, xlo, first, last):
                nc.tensor.matmul(dst, wh, xhi, start=first, stop=False)
                nc.tensor.matmul(dst, wh, xlo, start=False, stop=False)
                return nc.tensor.matmul(dst, wl, xhi, start=False, stop=last)

            def gate_up(it, p):
                s = p % 2
                e, half, m = (p // (2 * IC)) % 2, (p // IC) % 2, p % IC
                if p % (2 * IC) == 0:
                    n = it * 2 + p // (2 * IC) + 1
                    pe.wait_ge(whi_ready, n * PIECES)
                    pe.wait_ge(wlo_ready, n * PIECES)
                for src, ps in ((0, gate_ps), (1, up_ps)):
                    if not (isinstance(it, int) and it == 0 and p < 2):
                        pe.wait_ge((gate_done, up_done)[src], it * PER + p - 1)
                    for c in range(DK):
                        col = c * 2 * INNER + src * INNER + m * P
                        last = split_product(ps[s], whi[e][:, col:col + P], wlo[e][:, col:col + P],
                                             xh[:, c, half * HALF:(half + 1) * HALF],
                                             xl[:, c, half * HALF:(half + 1) * HALF], c == 0, c == DK - 1)
                    last.then_inc(gu_ready, 1)

            def down(it, p):
                e, m, s = (p // (2 * IC)) % 2, p % IC, p % 4
                if m == 0 and not (isinstance(it, int) and it == 0 and p == 0):
                    pe.wait_ge(y_added, it * (PER // IC * DK) + p // IC * DK)
                pe.wait_ge(al_ready, it * PER + p + 1)
                for c in range(DK):
                    col = GU + m * D + c * P
                    last = split_product(y_ps[c][:], whi[e][:, col:col + P], wlo[e][:, col:col + P],
                                         ah[:, s], al[:, s], m == 0, m == IC - 1)
                last.then_inc(down_done, 1)

            def step(it, p):
                if not beyond(it, p):
                    gate_up(it, p)
                if p >= 2 and not beyond(it, p - 2):
                    down(it, p - 2)

            for kind, at in order:
                job = (kind, at)
                if kind in RELEASES:
                    claim(job)
                if kind == "tok":
                    if at == 0:
                        pe.wait_ge(wtok_in, 16)
                    pe.wait_ge(patch_in[at % 4], 16 * (at // 4 + 1))
                    for k in range(FK):
                        last = nc.tensor.matmul(bank(job)[:, 0:D], patches[:, at % 4, k, :], wtok[:, k // 3, k % 3, :],
                                                start=(k == 0), stop=(k == FK - 1))
                    last.then_inc(ready, 1)
                elif kind in ("x1T", "x2T", "yT"):
                    if kind == "x1T":
                        pe.wait_ge(x1_ready, at + 1)
                        src = x1[:, at]
                        if at == 0:
                            pe.wait_ge(const_in, 16)
                    elif kind == "x2T":
                        pe.wait_ge(x2_ready, at + 1)
                        src = x2[:, at % 2]
                    else:
                        pe.wait_ge(y_ready, 4 * (at + 1))
                        src = yn[:, at % 2]
                    for c in range(DK):
                        last = nc.tensor.transpose(bank(job)[:, c * P:(c + 1) * P], src[:, c * P:(c + 1) * P], ident)
                    last.then_inc(ready, 1)
                elif kind in ("q", "qs", "k", "ks"):
                    half, c = at
                    if kind == "q" and c == 0:
                        if half == 0:
                            pe.wait_ge(wqh_ready, 1)
                            pe.wait_ge(wql_ready, 1)
                        for t in range(half * TPH, half * TPH + TPH):
                            taken(pe, ("x1T", t))
                    col = ("q", "qs", "k", "ks").index(kind) * D + c * P
                    for k in range(DK):
                        last = split_product(bank(job)[:], wqh[:, k, col:col + P], wql[:, k, col:col + P],
                                             xh[:, k, half * HALF:(half + 1) * HALF],
                                             xl[:, k, half * HALF:(half + 1) * HALF], k == 0, k == DK - 1)
                    last.then_inc(ready, 1)
                elif kind in ("v", "logits"):
                    if kind == "logits":
                        if at == 0:
                            pe.wait_ge(rw_ready, 2)
                        taken(pe, ("x2T", at))
                        wh, wl, n = rwh, rwl, EXPERTS
                    else:
                        wh, wl, n = wqh[:, :, 4 * D:5 * D], wql[:, :, 4 * D:5 * D], D
                    for k in range(DK):
                        a_h, a_l = xh[:, k, at * P:(at + 1) * P], xl[:, k, at * P:(at + 1) * P]
                        last = split_product(bank(job)[:, 0:n], a_h, a_l, wh[:, k, :], wl[:, k, :],
                                             k == 0, k == DK - 1)
                    last.then_inc(ready, 1)
                elif kind == "scores":
                    half, i0 = at // TPH, at % TPH * P
                    if at % TPH == 0:
                        for c in range(DK):
                            taken(pe, ("q", (half, c)))
                            taken(pe, ("k", (half, c)))
                        pe.wait_ge(roped, 4 * (half + 1))
                    if at >= 1:
                        pe.wait_ge(y_ready, 4 * at)
                    for c in range(DK):
                        for j in range(4):
                            for i in range(4):
                                rows = slice(32 * i, 32 * i + 32)
                                cols = slice(i0 + 32 * j, i0 + 32 * j + 32)
                                dst = scores[32 * j:32 * j + 32, i, c * 64:c * 64 + 64]
                                nc.tensor.matmul(dst, kr[rows, c, cols], qz[rows, c, :, cols], start=True, stop=True)
                                dst = scores[32 * j:32 * j + 32, i, 128 + c * 64:128 + c * 64 + 64]
                                last = nc.tensor.matmul(dst, qn[rows, c, cols], kz[rows, c, :, cols],
                                                        start=True, stop=True)
                    last.then_inc(scored, 1)
                elif kind == "mix":
                    pe.wait_ge(p_ready, at + 1)
                    if at % TPH == 0:
                        for t in range(at, at + TPH):
                            taken(pe, ("v", t))
                    for i in range(4):
                        for cs in range(4):
                            head = (cs // 2) * 8 + i * 2 + cs % 2
                            for j in range(4):
                                rows = slice(32 * j, 32 * j + 32)
                                col = 256 + (i * 4 + cs) * DH
                                last = nc.tensor.matmul(scores[rows, j, col:col + DH],
                                                        p_sb[rows, at % 2, i, cs * 32:cs * 32 + 32],
                                                        v[rows, at % TPH, head * DH:(head + 1) * DH],
                                                        start=True, stop=True)
                    last.then_inc(mixed, 1)
                elif kind == "proj":
                    if at == 0:
                        pe.wait_ge(small_in, 16 * 7)
                    taken(pe, ("yT", at))
                    for c in range(DK):
                        last = nc.tensor.matmul(bank(job)[:, 0:D], yt[:, at % 2, c, :], wo[:, c, :],
                                                start=(c == 0), stop=(c == DK - 1))
                    last.then_inc(ready, 1)
            for t in range(NT):
                taken(pe, ("x2T", t))
            pe.wait_ge(y_ready, 4 * NT)
            gate_up(0, 0)
            gate_up(0, 1)
            pe.wait_ge(parts_ready, 1)
            pe.wait_ge(identb_ready, 1)
            claim(("cT", 0))
            cb = bank(("cT", 0))[:].bitcast(BF16)
            for t in range(NT):
                last = nc.tensor.transpose(cb[0:3 * EXPERTS, t * P:(t + 1) * P],
                                           parts[:, t].rearrange("p a b -> p (a b)"), identb[:])
            last.then_inc(ready, 1)
            for half in range(2):
                claim(("cTf", half))
                for i in range(TPH):
                    last = nc.tensor.transpose(bank(("cTf", half))[0:EXPERTS, i * P:(i + 1) * P],
                                               comb[:, half * TPH + i], ident)
                last.then_inc(ready, 1)
            for half in range(2):
                taken(pe, ("cTf", half))
                for c in range(DK):
                    job = ("bias", (c, half))
                    claim(job)
                    nc.tensor.matmul(bank(job)[:], bdown[:, c * P:(c + 1) * P], cTf[:, half * HALF:(half + 1) * HALF],
                                     start=True, stop=True).then_inc(ready, 1)
            taken(pe, ("cT", 0))
            pe.wait_ge(cz_ready, 1)
            for e in range(EXPERTS):
                for half in range(2):
                    job = ("share", (e, half))
                    claim(job)
                    nc.tensor.matmul(bank(job)[:], sel[:, e], cT[:, half * HALF:(half + 1) * HALF],
                                     start=True, stop=True).then_inc(ready, 1)
            taken(pe, ("share", (EXPERTS - 1, 0)))
            taken(pe, ("share", (EXPERTS - 1, 1)))
            taken(pe, ("share", (EXPERTS - 2, 0)))
            taken(pe, ("share", (EXPERTS - 2, 1)))
            with pe.Fori(0, LAST) as it:
                for p in range(2, 2 + PER):
                    step(it, p)
            for p in range(2, PER + 2):
                step(LAST, p)
            for t in range(NT):
                claim(("out", t))
                pe.wait_ge(y_added, EXPERTS * 2 * DK)
                for c in range(DK):
                    last = nc.tensor.transpose(bank(("out", t))[:, c * P:(c + 1) * P],
                                               yacc[:, c, t * P:(t + 1) * P], ident)
                last.then_inc(ready, 1)

        @block.scalar
        def _(act_eng):
            def split_high(slot, k):
                nc.scalar.copy(whi[slot][:, k * PIECE:(k + 1) * PIECE],
                               raw[slot][:, k * PIECE:(k + 1) * PIECE]).then_inc(whi_ready, 1)

            act_eng.wait_ge(const_in, 16)
            nc.scalar.copy(identb[:], ident).then_inc(identb_ready, 1)
            act_eng.wait_ge(wqkv_in, 16)
            nc.scalar.copy(halves[:, 0:DK * QKV], raw[1][:, 0:DK * QKV]).then_inc(wqh_ready, 1)
            act_eng.wait_ge(small_in, 16 * 7)
            nc.scalar.copy(rwh[:], rw[:]).then_inc(rw_ready, 1)
            for kind, at in order:
                job = (kind, at)
                if kind in ("x1T", "x2T"):
                    arrived(act_eng, job)
                    nc.scalar.copy(xh[:, :, at * P:(at + 1) * P],
                                   bank(job)[:, 0:D].rearrange("p (c n) -> p c n", c=DK))\
                        .then_inc(xhi_ready if kind == "x1T" else x2hi_ready, 1)
                elif kind == "q":
                    half, c = at
                    arrived(act_eng, job)
                    if half:
                        act_eng.wait_ge(scored, TPH)
                    nc.scalar.copy(qn[:, c], bank(job)[:]).then_inc(freed(job), 1)
                elif kind == "k":
                    half, c = at
                    arrived(act_eng, job)
                    nc.scalar.activation(kz[:, c, 0], bank(job)[:], ACT.Copy, scale=even)
                    nc.scalar.activation(kz[:, c, 1], bank(job)[:], ACT.Copy, scale=odd).then_inc(freed(job), 1)
                elif kind == "v":
                    arrived(act_eng, job)
                    if at == TPH:
                        act_eng.wait_ge(mixed, TPH)
                    nc.scalar.copy(v[:, at % TPH], bank(job)[:, 0:D]).then_inc(freed(job), 1)
                elif kind == "scores":
                    act_eng.wait_ge(scored, at + 1)
                    if at >= 2:
                        act_eng.wait_ge(den_ready, at - 1)
                    nc.scalar.activation(e_sb[:, at % 2], scores[:, :, 0:256].rearrange("p i (y n) -> p i y n", y=2),
                                         ACT.Exp, scale=SCALE).then_inc(exped, 1)
                elif kind == "yT":
                    arrived(act_eng, job)
                    if at >= 2:
                        arrived(act_eng, ("proj", at - 2))
                    nc.scalar.copy(yt[:, at % 2], bank(job)[:, 0:D].rearrange("p (c n) -> p c n", c=DK))\
                        .then_inc(freed(job), 1)
                elif kind == "split":
                    if at == 0:
                        act_eng.wait_ge(raw_in[0], 16)
                    split_high(0, at)
            act_eng.wait_ge(lsub_ready, 1)
            nc.scalar.activation(ex[:], ex[:], ACT.Exp).then_inc(ex_ready, 1)
            arrived(act_eng, ("cT", 0))
            act_eng.wait_ge(cz_ready, 1)
            nc.scalar.copy(cT[0:3 * EXPERTS, :], bank(("cT", 0))[:].bitcast(BF16)[0:3 * EXPERTS, :])\
                .then_inc(freed(("cT", 0)), 1)
            for e in range(EXPERTS):
                job = ("share", (e, 0))
                arrived(act_eng, job)
                nc.scalar.copy(shares[:, e * TOK:e * TOK + HALF], bank(job)[:]).then_inc(freed(job), 1)

            def step(it, p):
                if beyond(it, p):
                    return
                known = isinstance(it, int)
                s = p % 2
                act_eng.wait_ge(gate_done, it * PER + p + 1)
                if not (known and it == 0 and p < 2):
                    act_eng.wait_ge(s_done, it * PER + p - 1)
                nc.scalar.activation(tanh[:, s], gate[:, s], ACT.Tanh, scale=ALPHA / 2).then_inc(tanh_done, 1)
                piece = split_piece(p)
                if piece and not (known and it == LAST and p >= 2 * IC):
                    slot, k = piece
                    if k == 0:
                        n = p // (2 * IC) + 1 + it * 2
                        act_eng.wait_ge(raw_in[slot], (it + (p // (2 * IC) + 1) // 2) * 16 + 16)
                        if not (known and it == 0 and p < 2 * IC):
                            act_eng.wait_ge(down_done, (n - 1) * (2 * IC))
                    split_high(slot, k)
                act_eng.wait_ge(a_done, it * PER + p + 1)
                if not (known and it == 0 and p < 4):
                    act_eng.wait_ge(down_done, it * PER + p - 3)
                nc.scalar.copy(ah[:, p % 4], act[:, s]).then_inc(ah_ready, 1)

            loop(act_eng, step, 8)

        @block.gpsimd
        def _(pool):
            links = [0]

            def link(ins):
                links[0] += 1
                ins.then_inc(pchain, 1)
                pool.wait_ge(pchain, links[0])

            def split_low(slot, k):
                cols = slice(k * PIECE, (k + 1) * PIECE)
                nc.gpsimd.tensor_tensor(wlo[slot][:, cols], raw[slot][:, cols], whi[slot][:, cols].bitcast(F32),
                                        ALU.subtract).then_inc(wlo_ready, 1)

            def split_bias(slot):
                nc.gpsimd.tensor_tensor(bias[slot][:], raw[slot][:, WCOLS:WROW], offset[:], ALU.add)\
                    .then_inc(bias_ready, 1)

            nc.gpsimd.memset(power[:], -0.5)
            nc.gpsimd.memset(offset[:, 0:IC], 0.0)
            link(nc.gpsimd.memset(offset[:, IC:2 * IC], 1.0))
            nc.gpsimd.memset(cT[:], 0.0).then_inc(cz_ready, 1)
            pool.wait_ge(wqkv_in, 16)
            pool.wait_ge(wqh_ready, 1)
            nc.gpsimd.tensor_tensor(halves[:, DK * QKV:2 * DK * QKV], raw[1][:, 0:DK * QKV],
                                    halves[:, 0:DK * QKV].bitcast(F32), ALU.subtract).then_inc(wql_ready, 1)
            pool.wait_ge(rw_ready, 1)
            nc.gpsimd.tensor_tensor(rwl[:], rw[:], rwh[:].bitcast(F32), ALU.subtract).then_inc(rw_ready, 1)

            def root(i, t):
                pool.wait_ge(var_ready[i], t + 1)
                nc.gpsimd.tensor_tensor(rstd[:, i, t], ve[:, i, t], power[:], ALU.pow).then_inc(rstd_ready[i], 1)

            for kind, at in order:
                if kind == "tok":
                    root(0, at)
                elif kind in ("qs", "ks"):
                    half, c = at
                    taken(pool, (kind[0], at))
                    taken(pool, (kind, at))
                    n = 2 * c + (kind == "ks")
                    b = n % 2
                    if half and n == 0:
                        pool.wait_ge(scored, TPH)
                    if kind == "qs":
                        link(nc.gpsimd.tensor_tensor(ropec[:, b], ropec[:, b], ropes[:, b], ALU.add))
                        nc.gpsimd.tensor_scalar(qz[:, c, 0], ropec[:, b], even, None, ALU.mult)
                        nc.gpsimd.tensor_scalar(qz[:, c, 1], ropec[:, b], odd, None, ALU.mult).then_inc(roped, 1)
                    else:
                        nc.gpsimd.tensor_tensor(kr[:, c], ropec[:, b], ropes[:, b], ALU.add).then_inc(roped, 1)
                elif kind == "proj":
                    root(1, at)
                elif kind == "norm2":
                    pool.wait_ge(zn_ready, at + 1)
                    link(nc.gpsimd.tensor_tensor(z[:, at % 2], z[:, at % 2], gamma[:], ALU.mult))
                    link(nc.gpsimd.tensor_tensor(z[:, at % 2], z[:, at % 2], beta[:], ALU.add))
                    nc.gpsimd.tensor_tensor(h[:, at], h[:, at], z[:, at % 2], ALU.add).then_inc(h1_ready, 1)
                elif kind == "norm3":
                    root(2, at)
                elif kind == "split":
                    if at == 0:
                        pool.wait_ge(raw_in[0], 16)
                        split_bias(0)
                    pool.wait_ge(whi_ready, at + 1)
                    split_low(0, at)

            def step(it, p):
                if beyond(it, p):
                    return
                known = isinstance(it, int)
                piece = split_piece(p)
                if piece and not (known and it == LAST and p >= 2 * IC):
                    slot, k = piece
                    n = it * 2 + p // (2 * IC) + 1
                    pool.wait_ge(whi_ready, n * PIECES + k + 1)
                    if k == 0:
                        if not (known and it == 0 and p < 2 * IC):
                            pool.wait_ge(up_done, (n - 1) * (2 * IC))
                        split_bias(slot)
                    split_low(slot, k)
                pool.wait_ge(ah_ready, it * PER + p + 1)
                nc.gpsimd.tensor_tensor(al[:, p % 4], act[:, p % 2], ah[:, p % 4].bitcast(F32), ALU.subtract)\
                    .then_inc(al_ready, 1)

            loop(pool, step, 8)

        @block.vector
        def _(dve):
            links = [0]

            def link(ins):
                links[0] += 1
                ins.then_inc(chain, 1)
                dve.wait_ge(chain, links[0])

            def spread(i, t, src):
                link(nc.vector.bn_stats(stat[:, i, t], src))
                link(nc.vector.bn_aggr(mv[:, i, t], stat[:, i, t]))
                nc.vector.tensor_scalar(ve[:, i, t], mv[:, i, t, 1:2], EPS, None, ALU.add).then_inc(var_ready[i], 1)

            def normal(i, t, dst, src):
                dve.wait_ge(rstd_ready[i], t + 1)
                return nc.vector.tensor_scalar(dst, src, mv[:, i, t, 0:1], rstd[:, i, t], ALU.subtract, ALU.mult)

            def table(col):
                return const[:, col:col + SEQ].unsqueeze(1).broadcast_to([P, HALF // SEQ, SEQ])

            dve.wait_ge(rows_in, 16 * (P // SEQ + 1))
            link(nc.vector.tensor_tensor(pos[:], pos[:], tokb[:], ALU.add))
            for kind, at in order:
                job = (kind, at)
                if kind == "tok":
                    arrived(dve, job)
                    nc.vector.tensor_tensor(h[:, at], bank(job)[:, 0:D], pos[:], ALU.add).then_inc(freed(job), 1)
                    taken(dve, job)
                    spread(0, at, h[:, at])
                elif kind == "norm1":
                    normal(0, at, x1[:, at], h[:, at]).then_inc(x1_ready, 1)
                elif kind in ("x1T", "x2T"):
                    dve.wait_ge(xhi_ready if kind == "x1T" else x2hi_ready, at + 1)
                    cols = slice(at * P, (at + 1) * P)
                    nc.vector.tensor_tensor(xl[:, :, cols], bank(job)[:, 0:D].rearrange("p (c n) -> p c n", c=DK),
                                            xh[:, :, cols].bitcast(F32), ALU.subtract).then_inc(freed(job), 1)
                elif kind in ("q", "qs", "k", "ks"):
                    half, c = at
                    if kind == "q" and half == 0 and c == 0:
                        dve.wait_ge(const_in, 16)
                    arrived(dve, job)
                    if kind in "qk":
                        dve.wait_ge(freed(job), through[number[job]] - 1)
                    n = 4 * half + 2 * c + (kind[0] == "k")
                    if n >= 2:
                        dve.wait_ge(roped, n - 1)
                    dst = (ropes if kind[1:] else ropec)[:, n % 2]
                    nc.vector.tensor_tensor(dst.rearrange("p (b s) -> p b s", s=SEQ),
                                            bank(job)[:].rearrange("p (b s) -> p b s", s=SEQ),
                                            table(C_SIN if kind[1:] else C_COS), ALU.mult).then_inc(freed(job), 1)
                elif kind == "mask":
                    b = at % 2
                    if at >= 2:
                        dve.wait_ge(mixed, at - 1)
                    dve.wait_ge(exped, at + 1)
                    same = const[:, C_MASK:C_MASK + 32].unsqueeze(1).unsqueeze(1).broadcast_to([P, 4, 4, 32])
                    nc.vector.tensor_tensor(p_sb[:, b].rearrange("p i (g n) -> p i g n", n=32),
                                            e_sb[:, b, :, 0].rearrange("p i (g n) -> p i g n", n=32),
                                            same, ALU.mult).then_inc(p_ready, 1)
                    plain = e_sb[:, b, :, 1].rearrange("p i (g n) -> p i g n", n=32)
                    link(nc.vector.tensor_tensor(plain, plain, same, ALU.mult))
                    link(nc.vector.tensor_reduce(den[:, b].rearrange("p (i g) -> p i g", g=4), plain, AX, ALU.add))
                    nc.vector.reciprocal(rden[:, b], den[:, b]).then_inc(den_ready, 1)
                elif kind == "mix":
                    b = at % 2
                    dve.wait_ge(mixed, at + 1)
                    dve.wait_ge(den_ready, at + 1)
                    if at >= 2:
                        arrived(dve, ("yT", at - 2))
                    for j in range(4):
                        rows = slice(32 * j, 32 * j + 32)
                        nc.vector.tensor_tensor(yn[rows, b].rearrange("p (g n) -> p g n", n=DH),
                                                scores[rows, j, 256:512].rearrange("p (g n) -> p g n", n=DH),
                                                rden[rows, b].unsqueeze(2).broadcast_to([32, HEADS, DH]),
                                                ALU.mult).then_inc(y_ready, 1)
                elif kind == "proj":
                    arrived(dve, job)
                    if at >= 2:
                        dve.wait_ge(h1_ready, at - 1)
                    nc.vector.tensor_tensor(z[:, at % 2], bank(job)[:, 0:D], x1[:, at], ALU.add)\
                        .then_inc(freed(job), 1)
                    taken(dve, job)
                    spread(1, at, z[:, at % 2])
                elif kind == "norm2":
                    normal(1, at, z[:, at % 2], z[:, at % 2]).then_inc(zn_ready, 1)
                elif kind == "norm3":
                    dve.wait_ge(h1_ready, at + 1)
                    spread(2, at, h[:, at])
                    if at >= 2:
                        arrived(dve, ("x2T", at - 2))
                    normal(2, at, x2[:, at % 2], h[:, at]).then_inc(x2_ready, 1)
                elif kind == "logits":
                    if at == 0:
                        dve.wait_ge(small_in, 16 * 7)
                    arrived(dve, job)
                    nc.vector.tensor_tensor(lg[:, at], bank(job)[:, 0:EXPERTS], rb[:], ALU.add)\
                        .then_inc(freed(job), 1)
            for t in range(NT - RING, NT):
                taken(dve, ("logits", t))
            link(nc.vector.tensor_reduce(lmax[:], lg[:], AX, ALU.max))
            nc.vector.tensor_tensor(ex[:], lg[:], lmax[:].unsqueeze(2).broadcast_to([P, NT, EXPERTS]),
                                    ALU.subtract).then_inc(lsub_ready, 1)
            grid = [P, NT, EXPERTS, EXPERTS]
            other, own = lg[:].unsqueeze(2).broadcast_to(grid), lg[:].unsqueeze(3).broadcast_to(grid)
            above = pair[:, 0].rearrange("p (t a b) -> p t a b", t=NT, a=EXPERTS)
            equal = pair[:, 1].rearrange("p (t a b) -> p t a b", t=NT, a=EXPERTS)
            nc.vector.tensor_tensor(above, other, own, ALU.is_gt)
            link(nc.vector.tensor_tensor(equal, other, own, ALU.is_equal))
            before = const[:, C_TRI:C_COLS].unsqueeze(1).broadcast_to([P, NT, EXPERTS * EXPERTS])
            flat = pair[:, 1].rearrange("p (t n) -> p t n", t=NT)
            link(nc.vector.tensor_tensor(flat, flat, before, ALU.mult))
            link(nc.vector.tensor_tensor(above, above, equal, ALU.add))
            link(nc.vector.tensor_reduce(rank[:], above, AX, ALU.add))
            link(nc.vector.tensor_scalar(rank[:], rank[:], TOPK - 0.5, None, ALU.is_lt))
            dve.wait_ge(ex_ready, 1)
            link(nc.vector.tensor_tensor(comb[:], ex[:], rank[:], ALU.mult))
            link(nc.vector.tensor_reduce(lmax[:], comb[:], AX, ALU.add))
            link(nc.vector.reciprocal(lmax[:], lmax[:]))
            link(nc.vector.tensor_tensor(comb[:], comb[:], lmax[:].unsqueeze(2).broadcast_to([P, NT, EXPERTS]),
                                         ALU.mult))
            link(nc.vector.tensor_copy(parts[:, :, 0], comb[:]))
            link(nc.vector.tensor_tensor(rest[:], comb[:], parts[:, :, 0], ALU.subtract))
            link(nc.vector.tensor_copy(parts[:, :, 1], rest[:]))
            link(nc.vector.tensor_tensor(rest[:], rest[:], parts[:, :, 1], ALU.subtract))
            nc.vector.tensor_copy(parts[:, :, 2], rest[:]).then_inc(parts_ready, 1)
            for half in range(2):
                job = ("cTf", half)
                arrived(dve, job)
                nc.vector.tensor_copy(cTf[:, half * HALF:(half + 1) * HALF], bank(job)[0:EXPERTS, :])\
                    .then_inc(freed(job), 1)
            for half in range(2):
                for c in range(DK):
                    job = ("bias", (c, half))
                    arrived(dve, job)
                    nc.vector.tensor_copy(yacc[:, c, half * HALF:(half + 1) * HALF], bank(job)[:])\
                        .then_inc(freed(job), 1)
            for half in range(2):
                for c in range(DK):
                    taken(dve, ("bias", (c, half)))
            for e in range(EXPERTS):
                job = ("share", (e, 1))
                arrived(dve, job)
                nc.vector.tensor_copy(shares[:, e * TOK + HALF:(e + 1) * TOK], bank(job)[:]).then_inc(freed(job), 1)
            for e in range(EXPERTS):
                taken(dve, ("share", (e, 0)))
                taken(dve, ("share", (e, 1)))

            def add_up(it, p):
                unit = it * (PER // IC) + p // IC - 1
                half = (p // IC - 1) % 2
                dve.wait_ge(down_done, unit * IC + IC)
                dve.wait_ge(y_added, unit * DK) if not (isinstance(unit, int) and unit == 0) else None
                for c in range(DK):
                    dst = yacc[:, c, half * HALF:(half + 1) * HALF]
                    nc.vector.tensor_tensor(dst, y_ps[c][:], dst, ALU.add).then_inc(y_added, 1)

            def step(it, p):
                known = isinstance(it, int)
                if p >= IC + 2 and p % IC == 2:
                    add_up(it, p)
                if beyond(it, p):
                    return
                s, e, half, m = p % 2, (p // (2 * IC)) % 2, (p // IC) % 2, p % IC
                n = it * PER + p
                if p % (2 * IC) == 0:
                    dve.wait_ge(bias_ready, it * 2 + p // (2 * IC) + 1)
                if not (known and it == 0 and p < 2):
                    dve.wait_ge(al_ready, n - 1)
                dve.wait_ge(gu_ready, n * 2 + 1)
                nc.vector.tensor_scalar(gate[:, s], gate_ps[s], bias[e][:, m:m + 1], LIMIT, ALU.add, ALU.min)\
                    .then_inc(gate_done, 1)
                dve.wait_ge(gu_ready, n * 2 + 2)
                nc.vector.tensor_scalar(up[:, s], up_ps[s], bias[e][:, IC + m:IC + m + 1], LIMIT + 1, ALU.add,
                                        ALU.min).then_inc(up_done, 1)
                dve.wait_ge(tanh_done, n + 1)
                nc.vector.scalar_tensor_tensor(out=gate[:, s], in0=tanh[:, s], scalar=1.0, in1=gate[:, s],
                                               op0=ALU.add, op1=ALU.mult).then_inc(s_done, 1)
                dve.wait_ge(s_done, n + 1)
                nc.vector.scalar_tensor_tensor(out=up[:, s], in0=up[:, s], scalar=1.0 - LIMIT, in1=gate[:, s],
                                               op0=ALU.max, op1=ALU.mult).then_inc(m_done, 1)
                dve.wait_ge(m_done, n + 1)
                first = (it * 2 + p // (2 * IC)) * TOK + half * HALF
                nc.vector.tensor_tensor(act[:, s], up[:, s], shares[:, bass.ds(first, HALF)], ALU.mult)\
                    .then_inc(a_done, 1)

            loop(dve, step, 6)
            for t in range(NT):
                job = ("out", t)
                arrived(dve, job)
                if t >= 2:
                    dve.wait_ge(out_done[t % 2], 16 * (t // 2))
                nc.vector.tensor_tensor(ot[:, t % 2], bank(job)[:, 0:D], h[:, t], ALU.add).then_inc(freed(job), 1)
                taken(dve, job)
                dve.sem_inc(ot_ready, 1)


def constants():
    c = np.zeros((P, C_COLS), np.float32)
    c[:, C_ID:C_ID + P] = np.eye(P)
    p = np.arange(P)
    c[:, C_MASK:C_MASK + 32] = (p[:, None] % 32) // SEQ == np.arange(32)[None, :] // SEQ
    c[:, C_EVEN] = p // DH % 2 == 0
    c[:, C_ODD] = p // DH % 2 == 1
    i = np.arange(1, DH // 2 + 1, dtype=np.float32)
    theta = np.repeat(np.float32(1000.0) ** (np.float32(-2.0) * i / np.float32(DH)), 2)
    args = np.arange(1, SEQ + 1, dtype=np.float32)[:, None] * theta[None, :]
    sign = np.where(np.arange(DH) % 2 == 0, -1, 1).astype(np.float32)
    c[:, C_COS:C_COS + SEQ] = np.tile(np.cos(args).T, (P // DH, 1))
    c[:, C_SIN:C_SIN + SEQ] = np.tile((np.sin(args) * sign).T, (P // DH, 1))
    e = np.arange(EXPERTS)
    c[:, C_TRI:] = (e[None, :] < e[:, None]).reshape(1, -1)
    return c


def kernel(x, L0_tok_W, L0_tok_b, L0_tok_pos_emb, L0_attn_w_in, L0_attn_w_out, L0_attn_ln_gamma, L0_attn_ln_beta,
           L0_ffn_router_weight, L0_ffn_router_bias, L0_ffn_gate_up_proj, L0_ffn_gate_up_proj_bias, L0_ffn_down_proj,
           L0_ffn_down_proj_bias):
    import ml_dtypes
    import concourse.bacc as bacc
    from concourse.bass_utils import run_bass_kernel_spmd

    def rows(w, chunks):
        return w.reshape(chunks, P, -1).transpose(1, 0, 2)

    x = np.asarray(x).reshape(IMAGES, CH, GRID, PS, GRID, PS).transpose(1, 3, 5, 0, 2, 4).reshape(FK, P, NT, P)
    x = x.transpose(2, 1, 0, 3).reshape(NT, P, FK * P)
    w_in = np.asarray(L0_attn_w_in)
    swap = np.arange(D) ^ 1
    q, k, v = w_in[0:D], w_in[D:2 * D], w_in[2 * D:]
    wqkv = rows(np.concatenate([q, q[swap], k, k[swap], v]).T, DK).reshape(P, DK * QKV)
    heads = np.arange(HEADS).reshape(DK, 4, 2).transpose(1, 0, 2).ravel()
    wo = np.asarray(L0_attn_w_out).T.reshape(HEADS, DH, D)[heads].reshape(D, D)
    gu = np.asarray(L0_ffn_gate_up_proj).transpose(0, 2, 1).reshape(EXPERTS, DK, P, 2 * INNER).transpose(0, 2, 1, 3)
    down = np.asarray(L0_ffn_down_proj).transpose(0, 2, 1).reshape(EXPERTS, IC, P, D).transpose(0, 2, 1, 3)
    gub = np.asarray(L0_ffn_gate_up_proj_bias).reshape(EXPERTS, 2 * IC, P).transpose(0, 2, 1)
    wffn = np.concatenate([gu.reshape(EXPERTS, P, -1), down.reshape(EXPERTS, P, -1), gub], axis=2)
    sel = np.zeros((P, EXPERTS, P), np.float32)
    for part in range(3):
        for e in range(EXPERTS):
            sel[part * EXPERTS + e, e] = 0.5
    arrays = {
        "x": x, "wtok": rows(np.asarray(L0_tok_W).T, FK), "tokb": np.asarray(L0_tok_b),
        "pos": np.asarray(L0_tok_pos_emb), "wqkv": wqkv, "wo": rows(wo, DK), "gamma": np.asarray(L0_attn_ln_gamma),
        "beta": np.asarray(L0_attn_ln_beta), "rw": rows(np.asarray(L0_ffn_router_weight).T, DK),
        "rb": np.asarray(L0_ffn_router_bias), "wffn": wffn, "bdown": np.asarray(L0_ffn_down_proj_bias),
        "const": constants(), "sel": sel.astype(ml_dtypes.bfloat16),
    }
    arrays = {n: np.ascontiguousarray(a) for n, a in arrays.items()}
    nc = bacc.Bacc("TRN2", target_bir_lowering=False, num_devices=1)
    args = [nc.dram_tensor(f"in_{n}", a.shape, mybir.dt.from_np(a.dtype), kind="ExternalInput").ap()
            for n, a in arrays.items()]
    out = nc.dram_tensor("out", [TOK, D], F32, kind="ExternalOutput").ap()
    build(nc, *args, out)
    r = run_bass_kernel_spmd(nc, [{f"in_{n}": a for n, a in arrays.items()}], core_ids=[0])
    return r.results[0]["out"].reshape(IMAGES, SEQ, D)
```

```python
from contextlib import ExitStack

import numpy as np

import concourse.bass as bass
from concourse import mybir

P = 128
ALU = mybir.AluOpType
ACT = mybir.ActivationFunctionType
AX = mybir.AxisListType.X
F32 = mybir.dt.float32
F32R = mybir.dt.float32r
BF16 = mybir.dt.bfloat16

IMAGES, CH, IMG, PS = 64, 3, 64, 16
GRID = IMG // PS
SEQ = GRID * GRID
TOK = IMAGES * SEQ
NT = TOK // P
HALF = TOK // 2
TPH = NT // 2
D = 256
DK = D // P
FEAT = CH * PS * PS
FK = FEAT // P
HEADS, DH = 16, 16
SCALE = 1.0 / 4.0
EXPERTS, INNER, TOPK = 8, 512, 4
IC = INNER // P
ALPHA, LIMIT = 1.702, 7.0
EPS = 1e-5
QKV = 5 * D
GU = DK * 2 * INNER
WCOLS = GU + IC * D
WROW = WCOLS + 2 * IC
PIECE = 512
PIECES = WCOLS // PIECE
GU_PIECES = GU // PIECE

C_ID, C_MASK, C_EVEN, C_ODD, C_COS, C_SIN, C_TRI = 0, 128, 160, 161, 162, 178, 194
C_COLS = C_TRI + EXPERTS * EXPERTS


def stages():
    def turn(t):
        return [("norm1", t), ("x1T", t)]

    def chunk(half, c, what):
        return [(kind, (half, c)) for kind in what]

    def values(half):
        return [("v", t) for t in range(half * TPH, half * TPH + TPH)]

    qq, kk = ("q", "qs"), ("k", "ks")
    order = [("tok", 0), ("tok", 1)] + turn(0) + [("wsplit", 0), ("tok", 2)] + turn(1) + [("wsplit", 1), ("tok", 3)]
    order += turn(2) + [("tok", 4)] + turn(3)
    for c in range(DK):
        order += chunk(0, c, qq + kk)
    order += values(0)
    while_weights = {0: [("tok", 5)] + turn(4), 1: [("tok", 7)] + turn(6), 2: chunk(1, 0, qq), 3: chunk(1, 0, kk),
                     4: values(1), 5: [("split", 0)], 6: [("logits", 0), ("split", 2)], 7: [("cT", 0), ("cTf", 0)]}
    while_values = {0: [("tok", 6)] + turn(5), 1: turn(7), 2: chunk(1, 1, qq), 3: chunk(1, 1, kk),
                    5: [("split", 1)], 6: [("lgT", 0), ("router", 0), ("split", 3), ("split", 4)],
                    7: [("bias", (0, 0)), ("bias", (1, 0)), ("split", 5)]}
    for t in range(NT):
        order += [("scores", t), ("mask", t)]
        if t >= 2:
            order += [("spread3", t - 2)]
        if t >= 1:
            order += [("yT", t - 1)]
        order += while_weights.get(t, [])
        if t >= 2:
            order += [("norm3", t - 2)]
        if t >= 1:
            order += [("proj", t - 1)]
        order += [("mix", t)]
        order += while_values.get(t, [])
        if t >= 1:
            order += [("norm2", t - 1)]
        if t >= 2:
            order += [("x2T", t - 2)]
    last = NT - 1
    order += [("spread3", last - 1), ("yT", last), ("norm3", last - 1), ("step", 0), ("proj", last),
              ("x2T", last - 1), ("step", 1), ("norm2", last), ("spread3", last), ("norm3", last), ("step", 2),
              ("x2T", last), ("step", 3), ("logits", 1), ("lgT", 1), ("router", 1), ("step", 4), ("cT", 1),
              ("cTf", 1), ("bias", (0, 1)), ("bias", (1, 1)), ("share1", 0), ("step", 5), ("step", 6), ("step", 7)]
    return order


RELEASES = {"tok": 1, "x1T": 1, "q": 2, "qs": 1, "k": 2, "ks": 1, "v": 1, "yT": 1, "proj": 1, "x2T": 1, "logits": 1,
            "lgT": 1, "cT": 1, "cTf": 1, "bias": 1, "out": 1}
RING = 4
LAG = 3


def build(nc, A_x, A_wtok, A_tokb, A_pos, A_wqkv, A_wo, A_gamma, A_beta, A_rw, A_rb, A_wffn, A_bdown, A_const,
          A_sel, out):
    order = stages()
    sums = [s for s in order if s[0] in ("qs", "ks")]
    jobs = [s for s in order if s[0] in RELEASES] + [("out", t) for t in range(NT)]
    number = {job: n for n, job in enumerate(jobs)}
    overlapped = {s for s in order[order.index(("step", 0)):] if s[0] in RELEASES}
    place, through, former, total, latest = {}, {}, {}, [0] * RING, [None] * RING
    for n, job in enumerate(jobs):
        b = RING - 1 if job in overlapped else job[1] % RING if job[0] == "out" else n % RING
        if job[0] == "out" and job[1] < TPH:
            b = 2
        former[job] = latest[b]
        total[b] += RELEASES[job[0]]
        place[job], through[job], latest[b] = b, total[b], job
    last_job = [[s for s in jobs if s[0] != "out" and place[s] == b][-1] for b in range(RING)]

    with ExitStack() as ctx:
        def sb(name, shape, dt=F32):
            return ctx.enter_context(nc.sbuf_tensor(name, shape, dt))

        def sem(name):
            return ctx.enter_context(nc.semaphore(name))

        banks = [ctx.enter_context(nc.psum_tensor(f"bank{i}", [P, 512], F32)) for i in range(RING)]
        scores = ctx.enter_context(nc.psum_tensor("scores", [P, 4, 512], F32))
        gate_ps, up_ps = [scores[:, 0, :], scores[:, 1, :]], [scores[:, 2, :], scores[:, 3, :]]
        y_ps = [banks[0], banks[1]]
        share_ps = [banks[2], banks[3]]

        const = sb("const", [P, C_COLS])
        ident = const[:, C_ID:C_ID + P]
        even, odd = const[:, C_EVEN:C_EVEN + 1], const[:, C_ODD:C_ODD + 1]
        sel = sb("sel", [P, EXPERTS, P], BF16)
        identb = sb("identb", [P, P], BF16)
        pos = sb("pos", [P, D])
        tokb = sb("tokb", [P, D])
        gamma = sb("gamma", [P, D])
        beta = sb("beta", [P, D])
        rb = sb("rb", [P, EXPERTS])
        rw = sb("rw", [P, DK, P])
        rwh = sb("rwh", [P, DK, P], F32R)
        rwl = sb("rwl", [P, DK, P], F32R)
        bdown = sb("bdown", [EXPERTS, D])
        wo = sb("wo", [P, DK, D])
        raw = [sb(f"raw{i}", [P, WROW]) for i in range(2)]
        patches = raw[0][:, 0:4 * FK * P].rearrange("p (b k n) -> p b k n", b=4, k=FK)
        bias = [sb(f"bias{i}", [P, 2 * IC]) for i in range(2)]
        whi = [sb(f"whi{i}", [P, WCOLS], F32R) for i in range(2)]
        wlo = [sb(f"wlo{i}", [P, WCOLS], F32R) for i in range(2)]
        xh = sb("xh", [P, DK, TOK], F32R)
        xl = sb("xl", [P, DK, TOK], F32R)
        h = sb("h", [P, NT, D])
        x1 = sb("x1", [P, NT, D])
        yacc = sb("yacc", [P, DK, TOK])
        wtok = yacc[:, :, 0:FK * D // DK].rearrange("p c (k n) -> p c k n", n=D)
        plain = [raw[1][:, 0:3 * DK * HALF], sb("plain_qk", [P, 3 * DK * HALF])[:]]
        qn = [a[:, 0:DK * HALF].rearrange("p (c n) -> p c n", c=DK) for a in plain]
        kz = [a[:, DK * HALF:].rearrange("p (c y n) -> p c y n", c=DK, y=2) for a in plain]
        kr = sb("kr", [P, DK, HALF])
        qz = [sb("qz", [P, DK, 2, HALF])[:], yacc[:].rearrange("p c (y n) -> p c y n", y=2)]
        v = sb("v", [P, TPH, D])
        yt = sb("yt", [P, 2, DK, P])
        x2 = sb("x2", [P, 2, D])
        halves = sb("halves", [P, 2 * DK * QKV], F32R)
        wqh = halves[:, 0:DK * QKV].rearrange("p (c n) -> p c n", c=DK)
        wql = halves[:, DK * QKV:2 * DK * QKV].rearrange("p (c n) -> p c n", c=DK)
        ah = halves[:, 0:2048].rearrange("p (b n) -> p b n", b=4)
        al = halves[:, 2048:4096].rearrange("p (b n) -> p b n", b=4)
        work = sb("work", [P, 10 * 512])
        wk = work[:, :].rearrange("p (s b n) -> p s b n", s=5, b=2)
        gate, tanh, up, act = wk[:, 0], wk[:, 1], wk[:, 2], wk[:, 3]
        e_sb = work[:, 0:2048].rearrange("p (b i y n) -> p b i y n", b=2, i=4, y=2)
        p_sb = work[:, 2048:3072].rearrange("p (b i n) -> p b i n", b=2, i=4)
        ropec = work[:, 3072:4096].rearrange("p (b n) -> p b n", b=2)
        ropes = work[:, 4096:5120].rearrange("p (b n) -> p b n", b=2)
        yn = sb("yn", [P, 2, D])
        z = sb("z", [P, 2, D])
        den = sb("den", [P, 2, HEADS])
        rden = sb("rden", [P, 2, HEADS])
        stat = sb("stat", [P, 3, NT, 6])
        mv = sb("mv", [P, 3, NT, 2])
        ve = sb("ve", [P, 3, NT, 1])
        rstd = sb("rstd", [P, 3, NT, 1])
        power = sb("power", [P, 1])
        offset = sb("offset", [P, 2 * IC])
        lg = sb("lg", [P, NT, EXPERTS])
        lmax = sb("lmax", [P, NT])
        ex = sb("ex", [P, NT, EXPERTS])
        above, equal = (a[:, 0:TPH * EXPERTS * EXPERTS] for a in (pos, tokb))
        rank = sb("rank", [P, NT, EXPERTS])
        comb = sb("comb", [P, NT, EXPERTS])
        rest = sb("rest", [P, NT, EXPERTS])
        parts = sb("parts", [P, NT, 3, EXPERTS], BF16)
        cT = sb("cT", [P, TOK], BF16)
        flat_x1 = x1[0:EXPERTS].rearrange("p t n -> p (t n)")
        cTf = [flat_x1[:, 0:HALF], flat_x1[:, 3 * HALF:4 * HALF]]
        lgT = [flat_x1[:, HALF:2 * HALF], flat_x1[:, 2 * HALF:3 * HALF]]

        wtok_in, const_in, rows_in, wqkv_in, small_in = (sem(n) for n in ("wtok_in", "const_in", "rows_in",
                                                                         "wqkv_in", "small_in"))
        patch_in = [sem(f"patch_in{i}") for i in range(4)]
        raw_in = [sem(f"raw_in{i}") for i in range(2)]
        ready = sem("ring_ready")
        free = [sem(f"ring_free{i}") for i in range(RING)]
        chain, pchain, cz_ready = sem("dve_chain"), sem("pool_chain"), sem("cz_ready")
        wqh_ready, rwh_ready, rwl_ready = sem("wqh_ready"), sem("rwh_ready"), sem("rwl_ready")
        wql_ready = [sem(f"wql_ready{i}") for i in range(DK)]
        share_ready = sem("share_ready")
        identb_ready = sem("identb_ready")
        var_ready = [sem(f"var_ready{i}") for i in range(3)]
        rstd_ready = [sem(f"rstd_ready{i}") for i in range(3)]
        x1_ready, xhi_ready, x2_ready, x2hi_ready = sem("x1_ready"), sem("xhi_ready"), sem("x2_ready"), sem("x2hi_ready")
        roped = sem("roped")
        scored, exped, p_ready, den_ready = sem("scored"), sem("exped"), sem("p_ready"), sem("den_ready")
        mixed, y_ready, zn_ready, h1_ready = sem("mixed"), sem("y_ready"), sem("zn_ready"), sem("h1_ready")
        lsub_ready, ex_ready, parts_ready = sem("lsub_ready"), sem("ex_ready"), sem("parts_ready")
        whi_ready, wlo_ready, bias_ready = sem("whi_ready"), sem("wlo_ready"), sem("bias_ready")
        gu_ready, gate_done, up_done, tanh_done = sem("gu_ready"), sem("gate_done"), sem("up_done"), sem("tanh_done")
        s_done, m_done, a_done = sem("s_done"), sem("m_done"), sem("a_done")
        ah_ready, al_ready, down_done, y_added = sem("ah_ready"), sem("al_ready"), sem("down_done"), sem("y_added")
        out_done = sem("out_done")

        def bank(job):
            return banks[place[job]]

        def arrived(eng, job):
            eng.wait_ge(ready, number[job] + 1)

        def freed(job):
            return free[place[job]]

        def taken(eng, job):
            eng.wait_ge(freed(job), through[job])

        block = ctx.enter_context(nc.Block())

        @block.sync
        def _(sp):
            sp.dma_start(wtok, A_wtok.rearrange("p (c k) n -> p c k n", c=DK)).then_inc(wtok_in, 16)
            sp.dma_start(patches[:, 0], A_x[0]).then_inc(patch_in[0], 16)
            sp.dma_start(patches[:, 1], A_x[1]).then_inc(patch_in[1], 16)
            sp.dma_start(pos[:], A_pos).then_inc(rows_in, 16)
            sp.dma_start(tokb[:], A_tokb.partition_broadcast(P)).then_inc(rows_in, 16)
            sp.dma_start(const[:], A_const).then_inc(const_in, 16)
            sp.dma_start(patches[:, 2], A_x[2]).then_inc(patch_in[2], 16)
            sp.dma_start(raw[1][:, 0:DK * QKV], A_wqkv).then_inc(wqkv_in, 16)
            sp.dma_start(patches[:, 3], A_x[3]).then_inc(patch_in[3], 16)
            for dst, src in ((rw, A_rw), (gamma, A_gamma.partition_broadcast(P)), (beta, A_beta.partition_broadcast(P)),
                             (rb, A_rb.partition_broadcast(P)), (wo, A_wo), (bdown, A_bdown), (sel, A_sel)):
                sp.dma_start(dst[:], src).then_inc(small_in, 16)
            for t in range(4, NT):
                arrived(sp, ("tok", t - 4))
                sp.dma_start(patches[:, t % 4], A_x[t]).then_inc(patch_in[t % 4], 16)
            arrived(sp, ("tok", NT - 1))
            sp.dma_start(raw[0][:], A_wffn[0]).then_inc(raw_in[0], 16)
            for k in range(DK):
                sp.wait_ge(wql_ready[k], 1)
            sp.wait_ge(scored, TPH)
            sp.dma_start(raw[1][:], A_wffn[1]).then_inc(raw_in[1], 16)
            with sp.Fori(1, EXPERTS // 2) as it:
                for i in range(2):
                    sp.wait_ge(wlo_ready, it * (2 * PIECES) + (i - 1) * PIECES)
                    sp.dma_start(raw[i][:], A_wffn[bass.ds(it * 2 + i, 1)].rearrange("e p n -> (e p) n"))\
                        .then_inc(raw_in[i], 16)
            for t in range(NT):
                taken(sp, ("out", t))
                sp.dma_start(out[t * P:(t + 1) * P, :], h[:, t]).then_inc(out_done, 16)
            sp.wait_ge(out_done, 16 * NT)

        PER = 2 * 2 * IC
        LAST = EXPERTS // 2 - 1
        FIRST = sum(kind == "step" for kind, _ in order)

        def loop(eng, step, output):
            with eng.Fori(0, LAST) as it:
                for p in range(FIRST, FIRST + PER):
                    step(it, p)
            for p in range(FIRST, PER + IC):
                step(LAST, p)
                if p >= PER:
                    output(p - PER)
            for t in range(IC, NT):
                output(t)

        def no_output(t):
            pass

        def beyond(it, p):
            return isinstance(it, int) and (it == LAST and p >= PER or it == 0 and p < 0)

        def begins(it, p, slots):
            return isinstance(it, int) and it == 0 and p < slots

        def split_piece(it, p):
            k = p % (2 * IC) - 2
            if k < 0 or isinstance(it, int) and it == LAST and p >= 2 * IC:
                return None
            return it * 2 + p // (2 * IC) + 1, (p // (2 * IC) + 1) % 2, k

        @block.tensor
        def _(pe):
            def claim(job):
                if former[job]:
                    taken(pe, former[job])

            def split_product(dst, wh, wl, xhi, xlo, first, last):
                nc.tensor.matmul(dst, wh, xhi, start=first, stop=False)
                nc.tensor.matmul(dst, wh, xlo, start=False, stop=False)
                return nc.tensor.matmul(dst, wl, xhi, start=False, stop=last)

            def gate_up(it, p):
                s = p % 2
                e, half, m = (p // (2 * IC)) % 2, (p // IC) % 2, p % IC
                if p % (2 * IC) == 0:
                    n = (it * 2 + p // (2 * IC)) * PIECES + GU_PIECES
                    pe.wait_ge(whi_ready, n)
                    pe.wait_ge(wlo_ready, n)
                for src, ps in ((0, gate_ps), (1, up_ps)):
                    if not begins(it, p, 2):
                        pe.wait_ge((gate_done, up_done)[src], it * PER + p - 1)
                    for c in range(DK):
                        col = c * 2 * INNER + src * INNER + m * P
                        last = split_product(ps[s], whi[e][:, col:col + P], wlo[e][:, col:col + P],
                                             xh[:, c, half * HALF:(half + 1) * HALF],
                                             xl[:, c, half * HALF:(half + 1) * HALF], c == 0, c == DK - 1)
                    last.then_inc(gu_ready, 1)

            def down(it, p):
                e, m, s = (p // (2 * IC)) % 2, p % IC, p % 4
                if p % (2 * IC) == 0:
                    n = (it * 2 + p // (2 * IC) + 1) * PIECES
                    pe.wait_ge(whi_ready, n)
                    pe.wait_ge(wlo_ready, n)
                if begins(it, p, 1):
                    taken(pe, last_job[0])
                    taken(pe, last_job[1])
                pe.wait_ge(al_ready, it * PER + p + 1)
                for c in range(DK):
                    if m == 0 and not begins(it, p, 1):
                        pe.wait_ge(y_added, it * (PER // IC * DK) + (p // IC - 1) * DK + c + 1)
                    col = GU + m * D + c * P
                    last = split_product(y_ps[c][:], whi[e][:, col:col + P], wlo[e][:, col:col + P],
                                         ah[:, s], al[:, s], m == 0, m == IC - 1)
                last.then_inc(down_done, 1)

            def share(it, unit):
                half = unit % 2
                if not begins(it, unit, 2):
                    pe.wait_ge(a_done, it * PER + (unit - 1) * IC)
                nc.tensor.matmul(share_ps[half][:], sel[:, bass.ds(it * 2 + unit // 2, 1)].rearrange("p e n -> p (e n)"),
                                 cT[:, half * HALF:(half + 1) * HALF], start=True, stop=True).then_inc(share_ready, 1)

            def step(it, p):
                if not beyond(it, p):
                    gate_up(it, p)
                if p % IC == 2 and p > IC and not beyond(it, p + IC):
                    share(it, p // IC + 1)
                if not beyond(it, p - LAG):
                    down(it, p - LAG)

            def output(t):
                job = ("out", t)
                claim(job)
                if t == 0:
                    pe.wait_ge(a_done, EXPERTS * 2 * IC - IC)
                    pe.wait_ge(y_added, EXPERTS * 2 * DK - DK)
                if t == TPH:
                    pe.wait_ge(a_done, EXPERTS * 2 * IC)
                    pe.wait_ge(y_added, EXPERTS * 2 * DK)
                for c in range(DK):
                    last = nc.tensor.transpose(bank(job)[:, c * P:(c + 1) * P], yacc[:, c, t * P:(t + 1) * P], ident)
                last.then_inc(ready, 1)

            for kind, at in order:
                job = (kind, at)
                if kind in RELEASES:
                    claim(job)
                if kind == "tok":
                    if at == 0:
                        pe.wait_ge(wtok_in, 16)
                    pe.wait_ge(patch_in[at % 4], 16 * (at // 4 + 1))
                    for k in range(FK):
                        last = nc.tensor.matmul(bank(job)[:, 0:D], patches[:, at % 4, k, :], wtok[:, k // 3, k % 3, :],
                                                start=(k == 0), stop=(k == FK - 1))
                    last.then_inc(ready, 1)
                elif kind in ("x1T", "x2T", "yT"):
                    if kind == "x1T":
                        pe.wait_ge(x1_ready, at + 1)
                        src = x1[:, at]
                        if at == 0:
                            pe.wait_ge(const_in, 16)
                    elif kind == "x2T":
                        pe.wait_ge(x2_ready, at + 1)
                        src = x2[:, at % 2]
                    else:
                        pe.wait_ge(y_ready, 4 * (at + 1))
                        src = yn[:, at % 2]
                    for c in range(DK):
                        last = nc.tensor.transpose(bank(job)[:, c * P:(c + 1) * P], src[:, c * P:(c + 1) * P], ident)
                    last.then_inc(ready, 1)
                elif kind in ("q", "qs", "k", "ks"):
                    half, c = at
                    if kind == "q" and c == 0:
                        if half == 0:
                            pe.wait_ge(wqh_ready, DK)
                            for k in range(DK):
                                pe.wait_ge(wql_ready[k], 1)
                        for t in range(half * TPH, half * TPH + TPH):
                            taken(pe, ("x1T", t))
                    col = ("q", "qs", "k", "ks").index(kind) * D + c * P
                    for k in range(DK):
                        last = split_product(bank(job)[:], wqh[:, k, col:col + P], wql[:, k, col:col + P],
                                             xh[:, k, half * HALF:(half + 1) * HALF],
                                             xl[:, k, half * HALF:(half + 1) * HALF], k == 0, k == DK - 1)
                    last.then_inc(ready, 1)
                elif kind == "v":
                    for k in range(DK):
                        a_h, a_l = xh[:, k, at * P:(at + 1) * P], xl[:, k, at * P:(at + 1) * P]
                        last = split_product(bank(job)[:, 0:D], a_h, a_l, wqh[:, k, 4 * D:5 * D],
                                             wql[:, k, 4 * D:5 * D], k == 0, k == DK - 1)
                    last.then_inc(ready, 1)
                elif kind == "scores":
                    half, i0 = at // TPH, at % TPH * P
                    if at % TPH == 0:
                        for c in range(DK):
                            taken(pe, ("q", (half, c)))
                            taken(pe, ("k", (half, c)))
                        pe.wait_ge(roped, 4 * (half + 1))
                    if at >= 1:
                        pe.wait_ge(y_ready, 4 * at)
                    for c in range(DK):
                        for j in range(4):
                            for i in range(4):
                                rows = slice(32 * i, 32 * i + 32)
                                cols = slice(i0 + 32 * j, i0 + 32 * j + 32)
                                dst = scores[32 * j:32 * j + 32, i, c * 64:c * 64 + 64]
                                nc.tensor.matmul(dst, kr[rows, c, cols], qz[half][rows, c, :, cols],
                                                 start=True, stop=True)
                                dst = scores[32 * j:32 * j + 32, i, 128 + c * 64:128 + c * 64 + 64]
                                last = nc.tensor.matmul(dst, qn[half][rows, c, cols], kz[half][rows, c, :, cols],
                                                        start=True, stop=True)
                    last.then_inc(scored, 1)
                elif kind == "mix":
                    pe.wait_ge(p_ready, at + 1)
                    taken(pe, ("v", at))
                    for i in range(4):
                        for cs in range(4):
                            head = (cs // 2) * 8 + i * 2 + cs % 2
                            for j in range(4):
                                rows = slice(32 * j, 32 * j + 32)
                                col = 256 + (i * 4 + cs) * DH
                                last = nc.tensor.matmul(scores[rows, j, col:col + DH],
                                                        p_sb[rows, at % 2, i, cs * 32:cs * 32 + 32],
                                                        v[rows, at % TPH, head * DH:(head + 1) * DH],
                                                        start=True, stop=True)
                    last.then_inc(mixed, 1)
                elif kind == "proj":
                    if at == 0:
                        pe.wait_ge(small_in, 16 * 7)
                    taken(pe, ("yT", at))
                    for c in range(DK):
                        last = nc.tensor.matmul(bank(job)[:, 0:D], yt[:, at % 2, c, :], wo[:, c, :],
                                                start=(c == 0), stop=(c == DK - 1))
                    last.then_inc(ready, 1)
                elif kind == "logits":
                    if at == 0:
                        pe.wait_ge(rwh_ready, 1)
                        pe.wait_ge(rwl_ready, 1)
                    for t in range(at * TPH, at * TPH + TPH):
                        taken(pe, ("x2T", t))
                    for k in range(DK):
                        cols = slice(at * HALF, (at + 1) * HALF)
                        last = split_product(bank(job)[:], rwh[:, k], rwl[:, k], xh[:, k, cols], xl[:, k, cols],
                                             k == 0, k == DK - 1)
                    last.then_inc(ready, 1)
                elif kind == "lgT":
                    taken(pe, ("logits", at))
                    for i in range(TPH):
                        last = nc.tensor.transpose(bank(job)[:, i * EXPERTS:(i + 1) * EXPERTS],
                                                   lgT[at][:, i * P:(i + 1) * P], ident[0:EXPERTS, 0:EXPERTS])
                    last.then_inc(ready, 1)
                elif kind == "cT":
                    pe.wait_ge(parts_ready, at + 1)
                    if at == 0:
                        pe.wait_ge(identb_ready, 1)
                    for i in range(TPH):
                        last = nc.tensor.transpose(bank(job)[:].bitcast(BF16)[0:3 * EXPERTS, i * P:(i + 1) * P],
                                                   parts[:, at * TPH + i].rearrange("p a b -> p (a b)"), identb[:])
                    last.then_inc(ready, 1)
                elif kind == "cTf":
                    for i in range(TPH):
                        last = nc.tensor.transpose(bank(job)[0:EXPERTS, i * P:(i + 1) * P],
                                                   comb[:, at * TPH + i], ident)
                    last.then_inc(ready, 1)
                elif kind == "bias":
                    c, half = at
                    taken(pe, ("cTf", half))
                    nc.tensor.matmul(bank(job)[:], bdown[:, c * P:(c + 1) * P], cTf[half],
                                     start=True, stop=True).then_inc(ready, 1)
                elif kind == "share1":
                    taken(pe, ("cT", 1))
                    taken(pe, last_job[3])
                    share(0, 1)
                elif kind == "step":
                    if at == 0:
                        pe.wait_ge(y_ready, 4 * NT)
                        taken(pe, ("cT", 0))
                        pe.wait_ge(cz_ready, 1)
                        taken(pe, last_job[2])
                        share(0, 0)
                    if at == IC:
                        for t in range(TPH, NT):
                            taken(pe, ("x2T", t))
                    step(0, at)
            loop(pe, step, output)

        @block.scalar
        def _(act_eng):
            def split_high(slot, k):
                nc.scalar.copy(whi[slot][:, k * PIECE:(k + 1) * PIECE],
                               raw[slot][:, k * PIECE:(k + 1) * PIECE]).then_inc(whi_ready, 1)

            def step(it, p):
                n, s = it * PER + p, p % 2
                if not beyond(it, p):
                    act_eng.wait_ge(gate_done, n + 1)
                    if not begins(it, p, 2):
                        act_eng.wait_ge(s_done, n - 1)
                    nc.scalar.activation(tanh[:, s], gate[:, s], ACT.Tanh, scale=ALPHA / 2).then_inc(tanh_done, 1)
                if not beyond(it, p - 1):
                    act_eng.wait_ge(a_done, n)
                    if not begins(it, p - 1, 4):
                        act_eng.wait_ge(down_done, n - 4)
                    nc.scalar.copy(ah[:, (p - 1) % 4], act[:, 1 - s]).then_inc(ah_ready, 1)
                piece = split_piece(it, p)
                if piece:
                    expert, slot, k = piece
                    if k == 0:
                        act_eng.wait_ge(raw_in[slot], (it + (p // (2 * IC) + 1) // 2) * 16 + 16)
                        if not begins(it, p, 2 * IC):
                            act_eng.wait_ge(gu_ready, (expert - 1) * (2 * IC * 2))
                    if k == GU_PIECES and not begins(it, p, 2 * IC):
                        act_eng.wait_ge(down_done, (expert - 1) * (2 * IC))
                    split_high(slot, k)

            for kind, at in order:
                job = (kind, at)
                if kind == "wsplit":
                    if at == 0:
                        act_eng.wait_ge(wqkv_in, 16)
                    nc.scalar.copy(wqh[:, at], raw[1][:, at * QKV:(at + 1) * QKV]).then_inc(wqh_ready, 1)
                elif kind in ("x1T", "x2T"):
                    arrived(act_eng, job)
                    nc.scalar.copy(xh[:, :, at * P:(at + 1) * P],
                                   bank(job)[:, 0:D].rearrange("p (c n) -> p c n", c=DK))\
                        .then_inc(xhi_ready if kind == "x1T" else x2hi_ready, 1)
                elif kind == "q":
                    half, c = at
                    arrived(act_eng, job)
                    nc.scalar.copy(qn[half][:, c], bank(job)[:]).then_inc(freed(job), 1)
                elif kind == "k":
                    half, c = at
                    arrived(act_eng, job)
                    if c == 0 and half == 0:
                        act_eng.wait_ge(const_in, 16)
                    nc.scalar.activation(kz[half][:, c, 0], bank(job)[:], ACT.Copy, scale=even)
                    nc.scalar.activation(kz[half][:, c, 1], bank(job)[:], ACT.Copy, scale=odd)\
                        .then_inc(freed(job), 1)
                elif kind == "v":
                    arrived(act_eng, job)
                    if at == TPH:
                        act_eng.wait_ge(mixed, TPH)
                    nc.scalar.copy(v[:, at % TPH], bank(job)[:, 0:D]).then_inc(freed(job), 1)
                elif kind == "scores":
                    act_eng.wait_ge(scored, at + 1)
                    if at >= 2:
                        act_eng.wait_ge(den_ready, at - 1)
                    nc.scalar.activation(e_sb[:, at % 2], scores[:, :, 0:256].rearrange("p i (y n) -> p i y n", y=2),
                                         ACT.Exp, scale=SCALE).then_inc(exped, 1)
                elif kind == "yT":
                    arrived(act_eng, job)
                    if at >= 2:
                        arrived(act_eng, ("proj", at - 2))
                    nc.scalar.copy(yt[:, at % 2], bank(job)[:, 0:D].rearrange("p (c n) -> p c n", c=DK))\
                        .then_inc(freed(job), 1)
                elif kind == "split":
                    if at == 0:
                        act_eng.wait_ge(const_in, 16)
                        nc.scalar.copy(identb[:], ident).then_inc(identb_ready, 1)
                        act_eng.wait_ge(small_in, 16 * 7)
                        nc.scalar.copy(rwh[:], rw[:]).then_inc(rwh_ready, 1)
                        act_eng.wait_ge(raw_in[0], 16)
                    split_high(0, at)
                elif kind == "logits":
                    arrived(act_eng, job)
                    nc.scalar.copy(lgT[at], bank(job)[0:EXPERTS, :]).then_inc(freed(job), 1)
                elif kind == "router":
                    act_eng.wait_ge(lsub_ready, at + 1)
                    tiles = slice(at * TPH, (at + 1) * TPH)
                    nc.scalar.activation(ex[:, tiles], ex[:, tiles], ACT.Exp).then_inc(ex_ready, 1)
                elif kind == "cT":
                    arrived(act_eng, job)
                    act_eng.wait_ge(cz_ready, 1)
                    nc.scalar.copy(cT[0:3 * EXPERTS, at * HALF:(at + 1) * HALF],
                                   bank(job)[:].bitcast(BF16)[0:3 * EXPERTS, 0:HALF]).then_inc(freed(job), 1)
                elif kind == "step":
                    step(0, at)
            loop(act_eng, step, no_output)

        @block.gpsimd
        def _(pool):
            links = [0]

            def link(ins):
                links[0] += 1
                ins.then_inc(pchain, 1)
                pool.wait_ge(pchain, links[0])

            def split_low(slot, k):
                cols = slice(k * PIECE, (k + 1) * PIECE)
                nc.gpsimd.tensor_tensor(wlo[slot][:, cols], raw[slot][:, cols], whi[slot][:, cols].bitcast(F32),
                                        ALU.subtract).then_inc(wlo_ready, 1)

            def split_bias(slot):
                nc.gpsimd.tensor_tensor(bias[slot][:], raw[slot][:, WCOLS:WROW], offset[:], ALU.add)\
                    .then_inc(bias_ready, 1)

            def root(i, t):
                pool.wait_ge(var_ready[i], t + 1)
                nc.gpsimd.tensor_tensor(rstd[:, i, t], ve[:, i, t], power[:], ALU.pow).then_inc(rstd_ready[i], 1)

            def step(it, p):
                n = it * PER + p
                piece = split_piece(it, p)
                if piece:
                    expert, slot, k = piece
                    pool.wait_ge(whi_ready, expert * PIECES + k + 1)
                    if k == 0:
                        if not begins(it, p, 2 * IC):
                            pool.wait_ge(up_done, (expert - 1) * (2 * IC))
                        split_bias(slot)
                    split_low(slot, k)
                if not beyond(it, p - 1):
                    pool.wait_ge(ah_ready, n)
                    nc.gpsimd.tensor_tensor(al[:, (p - 1) % 4], act[:, (p - 1) % 2], ah[:, (p - 1) % 4].bitcast(F32),
                                            ALU.subtract).then_inc(al_ready, 1)

            nc.gpsimd.memset(power[:], -0.5)
            nc.gpsimd.memset(offset[:, 0:IC], 0.0)
            link(nc.gpsimd.memset(offset[:, IC:2 * IC], 1.0))
            nc.gpsimd.memset(cT[:], 0.0).then_inc(cz_ready, 1)
            for kind, at in order:
                if kind == "tok":
                    root(0, at)
                elif kind == "wsplit" and at == 0:
                    pool.wait_ge(wqh_ready, at + 1)
                    nc.gpsimd.tensor_tensor(wql[:, at], raw[1][:, at * QKV:(at + 1) * QKV], wqh[:, at].bitcast(F32),
                                            ALU.subtract).then_inc(wql_ready[at], 1)
                elif kind in ("qs", "ks"):
                    half, c = at
                    taken(pool, (kind[0], at))
                    taken(pool, (kind, at))
                    b = "qk".index(kind[0])
                    if half and kind == "ks" and c == 0:
                        pool.wait_ge(scored, TPH)
                    if kind == "qs":
                        link(nc.gpsimd.tensor_tensor(ropec[:, b], ropec[:, b], ropes[:, b], ALU.add))
                        nc.gpsimd.tensor_scalar(qz[half][:, c, 0], ropec[:, b], even, 1.0, ALU.mult, ALU.mult)
                        nc.gpsimd.tensor_scalar(qz[half][:, c, 1], ropec[:, b], odd, 1.0, ALU.mult, ALU.mult)\
                            .then_inc(roped, 1)
                    else:
                        nc.gpsimd.tensor_tensor(kr[:, c], ropec[:, b], ropes[:, b], ALU.add).then_inc(roped, 1)
                elif kind == "proj":
                    root(1, at)
                elif kind == "norm2":
                    pool.wait_ge(zn_ready, at + 1)
                    link(nc.gpsimd.tensor_tensor(z[:, at % 2], z[:, at % 2], gamma[:], ALU.mult))
                    link(nc.gpsimd.tensor_tensor(z[:, at % 2], z[:, at % 2], beta[:], ALU.add))
                    nc.gpsimd.tensor_tensor(h[:, at], h[:, at], z[:, at % 2], ALU.add).then_inc(h1_ready, 1)
                elif kind == "spread3":
                    root(2, at)
                elif kind == "split":
                    if at == 0:
                        pool.wait_ge(rwh_ready, 1)
                        nc.gpsimd.tensor_tensor(rwl[:], rw[:], rwh[:].bitcast(F32), ALU.subtract)\
                            .then_inc(rwl_ready, 1)
                        pool.wait_ge(raw_in[0], 16)
                        split_bias(0)
                    pool.wait_ge(whi_ready, at + 1)
                    split_low(0, at)
                elif kind == "step":
                    step(0, at)
            loop(pool, step, no_output)

        @block.vector
        def _(dve):
            links = [0]

            def link(ins):
                links[0] += 1
                ins.then_inc(chain, 1)
                dve.wait_ge(chain, links[0])

            def spread(i, t, src):
                link(nc.vector.bn_stats(stat[:, i, t], src))
                link(nc.vector.bn_aggr(mv[:, i, t], stat[:, i, t]))
                nc.vector.tensor_scalar(ve[:, i, t], mv[:, i, t, 1:2], EPS, None, ALU.add).then_inc(var_ready[i], 1)

            def normal(i, t, dst, src):
                dve.wait_ge(rstd_ready[i], t + 1)
                return nc.vector.tensor_scalar(dst, src, mv[:, i, t, 0:1], rstd[:, i, t], ALU.subtract, ALU.mult)

            def table(col):
                return const[:, col:col + SEQ].unsqueeze(1).broadcast_to([P, HALF // SEQ, SEQ])

            def route(at):
                tiles = slice(at * TPH, (at + 1) * TPH)
                l, x, c, r, m = lg[:, tiles], ex[:, tiles], comb[:, tiles], rest[:, tiles], lmax[:, tiles]
                k = rank[:, tiles]
                taken(dve, ("lgT", at))
                link(nc.vector.tensor_reduce(m, l, AX, ALU.max))
                nc.vector.tensor_tensor(x, l, m.unsqueeze(2).broadcast_to([P, TPH, EXPERTS]),
                                        ALU.subtract).then_inc(lsub_ready, 1)
                grid = [P, TPH, EXPERTS, EXPERTS]
                other, own = l.unsqueeze(2).broadcast_to(grid), l.unsqueeze(3).broadcast_to(grid)
                by_pair = above[:].rearrange("p (t a b) -> p t a b", t=TPH, a=EXPERTS)
                nc.vector.tensor_tensor(by_pair, other, own, ALU.is_gt)
                link(nc.vector.tensor_tensor(equal[:].rearrange("p (t a b) -> p t a b", t=TPH, a=EXPERTS), other, own,
                                             ALU.is_equal))
                before = const[:, C_TRI:C_COLS].unsqueeze(1).broadcast_to([P, TPH, EXPERTS * EXPERTS])
                flat = equal[:].rearrange("p (t n) -> p t n", t=TPH)
                link(nc.vector.tensor_tensor(flat, flat, before, ALU.mult))
                link(nc.vector.tensor_tensor(above[:], above[:], equal[:], ALU.add))
                link(nc.vector.tensor_reduce(k, by_pair, AX, ALU.add))
                link(nc.vector.tensor_scalar(k, k, TOPK - 0.5, None, ALU.is_lt))
                dve.wait_ge(ex_ready, at + 1)
                link(nc.vector.tensor_tensor(c, x, k, ALU.mult))
                link(nc.vector.tensor_reduce(m, c, AX, ALU.add))
                link(nc.vector.reciprocal(m, m))
                link(nc.vector.tensor_tensor(c, c, m.unsqueeze(2).broadcast_to([P, TPH, EXPERTS]), ALU.mult))
                link(nc.vector.tensor_copy(parts[:, tiles, 0], c))
                link(nc.vector.tensor_tensor(r, c, parts[:, tiles, 0], ALU.subtract))
                link(nc.vector.tensor_copy(parts[:, tiles, 1], r))
                link(nc.vector.tensor_tensor(r, r, parts[:, tiles, 1], ALU.subtract))
                nc.vector.tensor_copy(parts[:, tiles, 2], r).then_inc(parts_ready, 1)

            def add_up(it, unit):
                half = unit % 2
                n = it * (PER // IC) + unit
                dve.wait_ge(down_done, n * IC + IC)
                if not begins(it, unit, 2):
                    dve.wait_ge(y_added, n * DK)
                for c in range(DK):
                    if begins(it, unit, 2):
                        taken(dve, ("bias", (c, half)))
                    dst = yacc[:, c, half * HALF:(half + 1) * HALF]
                    nc.vector.tensor_tensor(dst, y_ps[c][:], dst, ALU.add).then_inc(y_added, 1)

            def step(it, p):
                n, s, f = it * PER + p, p % 2, (p - 1) % 2
                if p % IC == LAG and not beyond(it, p - IC):
                    add_up(it, p // IC - 1)
                now, then = not beyond(it, p), not beyond(it, p - 1)
                b, m = bias[(p // (2 * IC)) % 2], p % IC
                if now:
                    if p % (2 * IC) == 0:
                        dve.wait_ge(bias_ready, it * 2 + p // (2 * IC) + 1)
                    dve.wait_ge(gu_ready, n * 2 + 1)
                    nc.vector.tensor_scalar(gate[:, s], gate_ps[s], b[:, m:m + 1], LIMIT, ALU.add, ALU.min)\
                        .then_inc(gate_done, 1)
                if then:
                    dve.wait_ge(s_done, n)
                    nc.vector.scalar_tensor_tensor(out=up[:, f], in0=up[:, f], scalar=1.0 - LIMIT, in1=gate[:, f],
                                                   op0=ALU.max, op1=ALU.mult).then_inc(m_done, 1)
                if now:
                    dve.wait_ge(gu_ready, n * 2 + 2)
                    if not begins(it, p, 2):
                        dve.wait_ge(a_done, n - 1)
                    nc.vector.tensor_scalar(up[:, s], up_ps[s], b[:, IC + m:IC + m + 1], LIMIT + 1, ALU.add,
                                            ALU.min).then_inc(up_done, 1)
                if then:
                    dve.wait_ge(m_done, n)
                    if not begins(it, p - 1, 2):
                        dve.wait_ge(al_ready, n - 2)
                    unit = (p - 1) // IC
                    dve.wait_ge(share_ready, it * (PER // IC) + unit + 1)
                    nc.vector.tensor_tensor(act[:, f], up[:, f], share_ps[unit % 2][:], ALU.mult).then_inc(a_done, 1)
                if now:
                    dve.wait_ge(tanh_done, n + 1)
                    nc.vector.scalar_tensor_tensor(out=gate[:, s], in0=tanh[:, s], scalar=1.0, in1=gate[:, s],
                                                   op0=ALU.add, op1=ALU.mult).then_inc(s_done, 1)

            def output(t):
                job = ("out", t)
                arrived(dve, job)
                nc.vector.tensor_tensor(h[:, t], bank(job)[:, 0:D], h[:, t], ALU.add).then_inc(freed(job), 1)

            dve.wait_ge(rows_in, 16 * 2)
            link(nc.vector.tensor_tensor(pos[:], pos[:], tokb[:], ALU.add))
            for kind, at in order:
                job = (kind, at)
                if kind == "tok":
                    arrived(dve, job)
                    nc.vector.tensor_tensor(h[:, at], bank(job)[:, 0:D], pos[:], ALU.add).then_inc(freed(job), 1)
                    taken(dve, job)
                    spread(0, at, h[:, at])
                elif kind == "norm1":
                    normal(0, at, x1[:, at], h[:, at]).then_inc(x1_ready, 1)
                elif kind == "wsplit" and at == 1:
                    dve.wait_ge(wqh_ready, at + 1)
                    nc.vector.tensor_tensor(wql[:, at], raw[1][:, at * QKV:(at + 1) * QKV], wqh[:, at].bitcast(F32),
                                            ALU.subtract).then_inc(wql_ready[at], 1)
                elif kind in ("x1T", "x2T"):
                    dve.wait_ge(xhi_ready if kind == "x1T" else x2hi_ready, at + 1)
                    cols = slice(at * P, (at + 1) * P)
                    nc.vector.tensor_tensor(xl[:, :, cols], bank(job)[:, 0:D].rearrange("p (c n) -> p c n", c=DK),
                                            xh[:, :, cols].bitcast(F32), ALU.subtract).then_inc(freed(job), 1)
                elif kind in ("q", "qs", "k", "ks"):
                    half, c = at
                    if kind == "q" and half == 0 and c == 0:
                        dve.wait_ge(const_in, 16)
                    arrived(dve, job)
                    if kind in "qk":
                        dve.wait_ge(freed(job), through[job] - 1)
                    earlier = [n for n, s in enumerate(sums[0:sums.index((kind[0] + "s", at))]) if s[0][0] == kind[0]]
                    if earlier:
                        dve.wait_ge(roped, earlier[-1] + 1)
                    dst = (ropes if kind[1:] else ropec)[:, "qk".index(kind[0])]
                    nc.vector.tensor_tensor(dst.rearrange("p (b s) -> p b s", s=SEQ),
                                            bank(job)[:].rearrange("p (b s) -> p b s", s=SEQ),
                                            table(C_SIN if kind[1:] else C_COS), ALU.mult).then_inc(freed(job), 1)
                elif kind == "mask":
                    b = at % 2
                    if at >= 2:
                        dve.wait_ge(mixed, at - 1)
                    dve.wait_ge(exped, at + 1)
                    same = const[:, C_MASK:C_MASK + 32].unsqueeze(1).unsqueeze(1).broadcast_to([P, 4, 4, 32])
                    nc.vector.tensor_tensor(p_sb[:, b].rearrange("p i (g n) -> p i g n", n=32),
                                            e_sb[:, b, :, 0].rearrange("p i (g n) -> p i g n", n=32),
                                            same, ALU.mult).then_inc(p_ready, 1)
                    plain = e_sb[:, b, :, 1].rearrange("p i (g n) -> p i g n", n=32)
                    link(nc.vector.tensor_tensor(plain, plain, same, ALU.mult))
                    link(nc.vector.tensor_reduce(den[:, b].rearrange("p (i g) -> p i g", g=4), plain, AX, ALU.add))
                    nc.vector.reciprocal(rden[:, b], den[:, b]).then_inc(den_ready, 1)
                elif kind == "mix":
                    b = at % 2
                    dve.wait_ge(mixed, at + 1)
                    dve.wait_ge(den_ready, at + 1)
                    if at >= 2:
                        arrived(dve, ("yT", at - 2))
                    for j in range(4):
                        rows = slice(32 * j, 32 * j + 32)
                        nc.vector.tensor_tensor(yn[rows, b].rearrange("p (g n) -> p g n", n=DH),
                                                scores[rows, j, 256:512].rearrange("p (g n) -> p g n", n=DH),
                                                rden[rows, b].unsqueeze(2).broadcast_to([32, HEADS, DH]),
                                                ALU.mult).then_inc(y_ready, 1)
                elif kind == "proj":
                    arrived(dve, job)
                    if at >= 2:
                        dve.wait_ge(h1_ready, at - 1)
                    nc.vector.tensor_tensor(z[:, at % 2], bank(job)[:, 0:D], x1[:, at], ALU.add)\
                        .then_inc(freed(job), 1)
                    taken(dve, job)
                    spread(1, at, z[:, at % 2])
                elif kind == "norm2":
                    normal(1, at, z[:, at % 2], z[:, at % 2]).then_inc(zn_ready, 1)
                elif kind == "spread3":
                    dve.wait_ge(h1_ready, at + 1)
                    spread(2, at, h[:, at])
                elif kind == "norm3":
                    if at >= 2:
                        arrived(dve, ("x2T", at - 2))
                    normal(2, at, x2[:, at % 2], h[:, at]).then_inc(x2_ready, 1)
                elif kind == "lgT":
                    if at == 0:
                        dve.wait_ge(small_in, 16 * 7)
                    arrived(dve, job)
                    nc.vector.tensor_tensor(lg[:, at * TPH:(at + 1) * TPH],
                                            bank(job)[:, 0:TPH * EXPERTS].rearrange("p (t e) -> p t e", t=TPH),
                                            rb[:].unsqueeze(1).broadcast_to([P, TPH, EXPERTS]), ALU.add)\
                        .then_inc(freed(job), 1)
                elif kind == "router":
                    route(at)
                elif kind == "cTf":
                    arrived(dve, job)
                    nc.vector.tensor_copy(cTf[at], bank(job)[0:EXPERTS, :])\
                        .then_inc(freed(job), 1)
                elif kind == "bias":
                    c, half = at
                    arrived(dve, job)
                    nc.vector.tensor_copy(yacc[:, c, half * HALF:(half + 1) * HALF], bank(job)[:])\
                        .then_inc(freed(job), 1)
                elif kind == "step":
                    if at == 0:
                        dve.wait_ge(roped, 4 * 2)
                    step(0, at)
            loop(dve, step, output)


def constants():
    c = np.zeros((P, C_COLS), np.float32)
    c[:, C_ID:C_ID + P] = np.eye(P)
    p = np.arange(P)
    c[:, C_MASK:C_MASK + 32] = (p[:, None] % 32) // SEQ == np.arange(32)[None, :] // SEQ
    c[:, C_EVEN] = p // DH % 2 == 0
    c[:, C_ODD] = p // DH % 2 == 1
    i = np.arange(1, DH // 2 + 1, dtype=np.float32)
    theta = np.repeat(np.float32(1000.0) ** (np.float32(-2.0) * i / np.float32(DH)), 2)
    args = np.arange(1, SEQ + 1, dtype=np.float32)[:, None] * theta[None, :]
    sign = np.where(np.arange(DH) % 2 == 0, -1, 1).astype(np.float32)
    c[:, C_COS:C_COS + SEQ] = np.tile(np.cos(args).T, (P // DH, 1))
    c[:, C_SIN:C_SIN + SEQ] = np.tile((np.sin(args) * sign).T, (P // DH, 1))
    e = np.arange(EXPERTS)
    c[:, C_TRI:] = (e[None, :] < e[:, None]).reshape(1, -1)
    return c


def kernel(x, L0_tok_W, L0_tok_b, L0_tok_pos_emb, L0_attn_w_in, L0_attn_w_out, L0_attn_ln_gamma, L0_attn_ln_beta,
           L0_ffn_router_weight, L0_ffn_router_bias, L0_ffn_gate_up_proj, L0_ffn_gate_up_proj_bias, L0_ffn_down_proj,
           L0_ffn_down_proj_bias):
    import ml_dtypes
    import concourse.bacc as bacc
    from concourse.bass_utils import run_bass_kernel_spmd

    def rows(w, chunks):
        return w.reshape(chunks, P, -1).transpose(1, 0, 2)

    x = np.asarray(x).reshape(IMAGES, CH, GRID, PS, GRID, PS).transpose(1, 3, 5, 0, 2, 4).reshape(FK, P, NT, P)
    x = x.transpose(2, 1, 0, 3).reshape(NT, P, FK * P)
    w_in = np.asarray(L0_attn_w_in)
    swap = np.arange(D) ^ 1
    q, k, v = w_in[0:D], w_in[D:2 * D], w_in[2 * D:]
    wqkv = rows(np.concatenate([q, q[swap], k, k[swap], v]).T, DK).reshape(P, DK * QKV)
    heads = np.arange(HEADS).reshape(DK, 4, 2).transpose(1, 0, 2).ravel()
    wo = np.asarray(L0_attn_w_out).T.reshape(HEADS, DH, D)[heads].reshape(D, D)
    gu = np.asarray(L0_ffn_gate_up_proj).transpose(0, 2, 1).reshape(EXPERTS, DK, P, 2 * INNER).transpose(0, 2, 1, 3)
    down = np.asarray(L0_ffn_down_proj).transpose(0, 2, 1).reshape(EXPERTS, IC, P, D).transpose(0, 2, 1, 3)
    gub = np.asarray(L0_ffn_gate_up_proj_bias).reshape(EXPERTS, 2 * IC, P).transpose(0, 2, 1)
    wffn = np.concatenate([gu.reshape(EXPERTS, P, -1), down.reshape(EXPERTS, P, -1), gub], axis=2)
    sel = np.zeros((P, EXPERTS, P), np.float32)
    for part in range(3):
        for e in range(EXPERTS):
            sel[part * EXPERTS + e, e] = 0.5
    rw = np.zeros((P, DK, P), np.float32)
    rw[:, :, 0:EXPERTS] = rows(np.asarray(L0_ffn_router_weight).T, DK)
    arrays = {
        "x": x, "wtok": rows(np.asarray(L0_tok_W).T, FK), "tokb": np.asarray(L0_tok_b),
        "pos": np.tile(np.asarray(L0_tok_pos_emb), (P // SEQ, 1)), "wqkv": wqkv, "wo": rows(wo, DK), "gamma": np.asarray(L0_attn_ln_gamma),
        "beta": np.asarray(L0_attn_ln_beta), "rw": rw,
        "rb": np.asarray(L0_ffn_router_bias), "wffn": wffn, "bdown": np.asarray(L0_ffn_down_proj_bias),
        "const": constants(), "sel": sel.astype(ml_dtypes.bfloat16),
    }
    arrays = {n: np.ascontiguousarray(a) for n, a in arrays.items()}
    nc = bacc.Bacc("TRN2", target_bir_lowering=False, num_devices=1)
    args = [nc.dram_tensor(f"in_{n}", a.shape, mybir.dt.from_np(a.dtype), kind="ExternalInput").ap()
            for n, a in arrays.items()]
    out = nc.dram_tensor("out", [TOK, D], F32, kind="ExternalOutput").ap()
    build(nc, *args, out)
    r = run_bass_kernel_spmd(nc, [{f"in_{n}": a for n, a in arrays.items()}], core_ids=[0])
    return r.results[0]["out"].reshape(IMAGES, SEQ, D)
```

```python
from contextlib import ExitStack

import numpy as np

import concourse.bass as bass
from concourse import mybir

P = 128
ALU = mybir.AluOpType
ACT = mybir.ActivationFunctionType
AX = mybir.AxisListType.X
F32 = mybir.dt.float32
F32R = mybir.dt.float32r
BF16 = mybir.dt.bfloat16

IMAGES, CH, IMG, PS = 64, 3, 64, 16
GRID = IMG // PS
SEQ = GRID * GRID
TOK = IMAGES * SEQ
NT = TOK // P
HALF = TOK // 2
TPH = NT // 2
D = 256
DK = D // P
FEAT = CH * PS * PS
FK = FEAT // P
HEADS, DH = 16, 16
SCALE = 1.0 / 4.0
EXPERTS, INNER, TOPK = 8, 512, 4
IC = INNER // P
ALPHA, LIMIT = 1.702, 7.0
EPS = 1e-5
QKV = 5 * D
GU = DK * 2 * INNER
WCOLS = GU + IC * D
WROW = WCOLS + 2 * IC
PIECE = 512
PIECES = WCOLS // PIECE
GU_PIECES = GU // PIECE

C_ID, C_MASK, C_EVEN, C_ODD, C_COS, C_SIN, C_TRI = 0, 128, 160, 161, 162, 178, 194
C_COLS = C_TRI + EXPERTS * EXPERTS


def stages():
    def chunk(half, c, what):
        return [(kind, (half, c)) for kind in what]

    qq, kk = ("q", "qs"), ("k", "ks")
    order = [("tok", 0), ("tok", 1), ("norm1", 0), ("tok", 2), ("wsplit", 0), ("wsplit", 1), ("norm1", 1), ("x1T", 0),
             ("tok", 3), ("norm1", 2), ("x1T", 1), ("tok", 4), ("norm1", 3), ("x1T", 2), ("tok", 5), ("x1T", 3)]
    for c in range(DK):
        order += chunk(0, c, qq + kk)
    order += [("v", t) for t in range(TPH)]
    while_scores = {0: [("norm1", 4), ("norm1", 5)], 1: [("norm1", 6)], 2: [("norm1", 7)]}
    while_weights = {0: [("x1T", 4), ("tok", 6)], 1: [("x1T", 5), ("tok", 7), ("x1T", 6)],
                     2: [("x1T", 7)] + chunk(1, 0, qq), 3: chunk(1, 1, qq) + chunk(1, 0, kk) + chunk(1, 1, kk),
                     4: [("v", 4), ("v", 5)], 5: [("v", 6), ("split", 0), ("split", 1)],
                     6: [("v", 7), ("split", 2), ("lgT", 0)],
                     7: [("cTf", 0), ("cT", 0), ("split", 5)]}
    before_mix = {5: [("logits", 0)], 6: [("split", 3), ("split", 4)]}
    for t in range(NT):
        if t == NT - 1:
            order += [("router", 0)]
        order += [("scores", t)]
        if t >= 2:
            order += [("spread3", t - 2)]
        if t >= 1:
            order += [("yT", t - 1)]
        order += while_scores.get(t, [])
        if t >= 2:
            order += [("norm3", t - 2)]
        order += [("mask", t)]
        if t >= 2:
            order += [("x2T", t - 2)]
        order += while_weights.get(t, [])
        if t >= 1:
            order += [("proj", t - 1)]
        order += before_mix.get(t, [])
        if t >= 1:
            order += [("norm2", t - 1)]
        order += [("den", t), ("mix", t)]
    last = NT - 1
    order += [("spread3", last - 1), ("norm3", last - 1), ("step", 0), ("yT", last), ("x2T", last - 1), ("proj", last),
              ("norm2", last), ("step", 1), ("spread3", last), ("norm3", last), ("step", 2), ("x2T", last),
              ("step", 3), ("logits", 1), ("step", 4), ("lgT", 1), ("router", 1), ("cTf", 1), ("cT", 1),
              ("step", 5), ("share1", 0), ("step", 6), ("step", 7)]
    return order


def tensor_stages(order):
    for late, step in (([("x2T", NT - 1)], 3), ([("cTf", 1), ("cT", 1)], 5)):
        order = [s for s in order if s not in late]
        at = order.index(("step", step)) + 1
        order = order[:at] + late + order[at:]
    return order


RELEASES = {"tok": 1, "x1T": 1, "q": 2, "qs": 1, "k": 2, "ks": 1, "v": 1, "yT": 1, "proj": 1, "x2T": 1, "logits": 1,
            "lgT": 1, "cT": 1, "cTf": 1, "mix": 4}
RING = 4
LAG = 3


def build(nc, A_x, A_wtok, A_tokb, A_pos, A_wqkv, A_wo, A_gamma, A_beta, A_rw, A_rb, A_wffn, A_bdown, A_const,
          A_sel, out):
    order = stages()
    pe_order = tensor_stages(order)
    sums = [s for s in order if s[0] in ("qs", "ks")]
    jobs = [s for s in pe_order if s[0] in RELEASES]
    shared = {p: {s for s in pe_order[pe_order.index(("step", p)):] if s[0] in RELEASES} for p in (0, LAG)}
    number = {job: n + 1 for n, job in enumerate(s for s in jobs if s[0] != "mix")}
    place, through, before, total = {}, {}, {}, [0] * RING
    turn = 0

    def put(job, used):
        place[job] = used
        before[job] = {b: total[b] for b in used}
        for b in used:
            total[b] += RELEASES[job[0]] // len(used)
        through[job] = {b: total[b] for b in used}

    for job in jobs:
        if job[0] == "mix":
            put(job, [(turn + b) % RING for b in range(RING)])
        elif job in shared[LAG]:
            put(job, [RING - 1])
        elif job in shared[0]:
            put(job, [(0, 1, RING - 1)[turn % 3]])
            turn += 1
        else:
            put(job, [turn % RING])
            turn += 1
    experts_from = list(total)

    with ExitStack() as ctx:
        def sb(name, shape, dt=F32):
            return ctx.enter_context(nc.sbuf_tensor(name, shape, dt))

        def sem(name):
            return ctx.enter_context(nc.semaphore(name))

        banks = [ctx.enter_context(nc.psum_tensor(f"bank{i}", [P, 512], F32)) for i in range(RING)]
        scores = ctx.enter_context(nc.psum_tensor("scores", [P, 4, 512], F32))
        gate_ps, up_ps = [scores[:, 0, :], scores[:, 1, :]], [scores[:, 2, :], scores[:, 3, :]]
        y_ps = [banks[0], banks[1]]
        share_ps = [banks[2], banks[3]]

        const = sb("const", [P, C_COLS])
        ident = const[:, C_ID:C_ID + P]
        even, odd = const[:, C_EVEN:C_EVEN + 1], const[:, C_ODD:C_ODD + 1]
        sel = sb("sel", [P, EXPERTS, P], BF16)
        identb = sb("identb", [P, P], BF16)
        pos = sb("pos", [P, D])
        tokb = sb("tokb", [P, D])
        gamma = sb("gamma", [P, D])
        beta = sb("beta", [P, D])
        rb = sb("rb", [P, EXPERTS])
        rw = sb("rw", [P, DK, P])
        rwh = sb("rwh", [P, DK, P], F32R)
        rwl = sb("rwl", [P, DK, P], F32R)
        bdown = sb("bdown", [EXPERTS, D])
        wo = sb("wo", [P, DK, D])
        raw = [sb(f"raw{i}", [P, WROW]) for i in range(2)]
        patches = raw[0][:, 0:4 * FK * P].rearrange("p (b k n) -> p b k n", b=4, k=FK)
        bias = [sb(f"bias{i}", [P, 2 * IC]) for i in range(2)]
        whi = [sb(f"whi{i}", [P, WCOLS], F32R) for i in range(2)]
        wlo = [sb(f"wlo{i}", [P, WCOLS], F32R) for i in range(2)]
        xh = sb("xh", [P, DK, TOK], F32R)
        xl = sb("xl", [P, DK, TOK], F32R)
        h = sb("h", [P, NT, D])
        x1 = sb("x1", [P, NT, D])
        yacc = sb("yacc", [P, DK, TOK])
        wtok = yacc[:, :, 0:FK * D // DK].rearrange("p c (k n) -> p c k n", n=D)
        plain = [raw[1][:, 0:3 * DK * HALF], sb("plain_qk", [P, 3 * DK * HALF])[:]]
        qn = [a[:, 0:DK * HALF].rearrange("p (c n) -> p c n", c=DK) for a in plain]
        kz = [a[:, DK * HALF:].rearrange("p (c y n) -> p c y n", c=DK, y=2) for a in plain]
        kr = sb("kr", [P, DK, HALF])
        qz = [sb("qz", [P, DK, 2, HALF])[:], yacc[:].rearrange("p c (y n) -> p c y n", y=2)]
        v = sb("v", [P, TPH, D])
        yt = sb("yt", [P, 2, DK, P])
        x2 = sb("x2", [P, 2, D])
        halves = sb("halves", [P, 2 * DK * QKV], F32R)
        wqh = halves[:, 0:DK * QKV].rearrange("p (c n) -> p c n", c=DK)
        wql = halves[:, DK * QKV:2 * DK * QKV].rearrange("p (c n) -> p c n", c=DK)
        ah = halves[:, 0:2048].rearrange("p (b n) -> p b n", b=4)
        al = halves[:, 2048:4096].rearrange("p (b n) -> p b n", b=4)
        work = sb("work", [P, 10 * 512])
        wk = work[:, :].rearrange("p (s b n) -> p s b n", s=5, b=2)
        gate, tanh, up, act = wk[:, 0], wk[:, 1], wk[:, 2], wk[:, 3]
        e_sb = work[:, 0:2048].rearrange("p (b i y n) -> p b i y n", b=2, i=4, y=2)
        p_sb = work[:, 2048:3072].rearrange("p (b i n) -> p b i n", b=2, i=4)
        ropec = work[:, 3072:4096].rearrange("p (b n) -> p b n", b=2)
        ropes = work[:, 4096:5120].rearrange("p (b n) -> p b n", b=2)
        yn = sb("yn", [P, 2, D])
        z = sb("z", [P, 2, D])
        den = sb("den", [P, 2, HEADS])
        rden = sb("rden", [P, 2, HEADS])
        stat = sb("stat", [P, 3, NT, 6])
        mv = sb("mv", [P, 3, NT, 2])
        ve = sb("ve", [P, 3, NT, 1])
        rstd = sb("rstd", [P, 3, NT, 1])
        power = sb("power", [P, 1])
        offset = sb("offset", [P, 2 * IC])
        lg = sb("lg", [P, NT, EXPERTS])
        lmax = sb("lmax", [P, NT])
        ex = sb("ex", [P, NT, EXPERTS])
        above, equal = (a[:, 0:TPH * EXPERTS * EXPERTS] for a in (pos, tokb))
        rank = sb("rank", [P, NT, EXPERTS])
        comb = sb("comb", [P, NT, EXPERTS])
        rest = sb("rest", [P, NT, EXPERTS])
        parts = sb("parts", [P, NT, 3, EXPERTS], BF16)
        cT = sb("cT", [P, TOK], BF16)
        flat_x1 = x1[0:EXPERTS].rearrange("p t n -> p (t n)")
        cTf = [flat_x1[:, 0:HALF], flat_x1[:, 3 * HALF:4 * HALF]]
        lgT = [flat_x1[:, HALF:2 * HALF], flat_x1[:, 2 * HALF:3 * HALF]]

        const_in, rows_in, wqkv_in, small_in = (sem(n) for n in ("const_in", "rows_in", "wqkv_in", "small_in"))
        wtok_in = [sem(f"wtok_in{c}") for c in range(DK)]
        patch_in = [sem(f"patch_in{i}") for i in range(4)]
        raw_in = [sem(f"raw_in{i}") for i in range(2)]
        ready = sem("ring_ready")
        free = [sem(f"ring_free{i}") for i in range(RING)]
        chain, pchain, cz_ready = sem("dve_chain"), sem("pool_chain"), sem("cz_ready")
        wqh_ready, rwh_ready, rwl_ready = sem("wqh_ready"), sem("rwh_ready"), sem("rwl_ready")
        wql_ready = [sem(f"wql_ready{i}") for i in range(DK)]
        share_ready, zeroed, last_al_ready = sem("share_ready"), sem("zeroed"), sem("last_al_ready")
        identb_ready = sem("identb_ready")
        var_ready = [sem(f"var_ready{i}") for i in range(3)]
        rstd_ready = [sem(f"rstd_ready{i}") for i in range(3)]
        x1_ready, xhi_ready = sem("x1_ready"), sem("xhi_ready")
        x2_ready, x2hi_ready = sem("x2_ready"), sem("x2hi_ready")
        roped = sem("roped")
        scored, exped, p_ready, den_ready = sem("scored"), sem("exped"), sem("p_ready"), sem("den_ready")
        mixed, plain_ready, zn_ready, h1_ready = sem("mixed"), sem("plain_ready"), sem("zn_ready"), sem("h1_ready")
        lsub_ready, ex_ready = sem("lsub_ready"), sem("ex_ready")
        comb_ready, parts_ready = sem("comb_ready"), sem("parts_ready")
        whi_ready, wlo_ready, bias_ready = sem("whi_ready"), sem("wlo_ready"), sem("bias_ready")
        gu_ready, gate_done, up_done, tanh_done = sem("gu_ready"), sem("gate_done"), sem("up_done"), sem("tanh_done")
        s_done, m_done, a_done = sem("s_done"), sem("m_done"), sem("a_done")
        ah_ready, al_ready, down_done, y_added = sem("ah_ready"), sem("al_ready"), sem("down_done"), sem("y_added")
        turned_ready, out_ready, out_done = sem("turned_ready"), sem("out_ready"), sem("out_done")

        def bank(job):
            return banks[place[job][0]]

        def arrived(eng, job):
            eng.wait_ge(ready, number[job])

        def freed(job):
            return free[place[job][0]]

        def taken(eng, job):
            for b in place[job]:
                eng.wait_ge(free[b], through[job][b])

        block = ctx.enter_context(nc.Block())

        @block.sync
        def _(sp):
            sp.dma_start(patches[:, 0], A_x[0]).then_inc(patch_in[0], 16)
            for c in range(DK):
                sp.dma_start(wtok[:, c], A_wtok[:, c * FK // DK:(c + 1) * FK // DK]).then_inc(wtok_in[c], 16)
            sp.dma_start(patches[:, 1], A_x[1]).then_inc(patch_in[1], 16)
            sp.dma_start(pos[:], A_pos).then_inc(rows_in, 16)
            sp.dma_start(tokb[:], A_tokb.partition_broadcast(P)).then_inc(rows_in, 16)
            sp.dma_start(const[:], A_const).then_inc(const_in, 16)
            sp.dma_start(patches[:, 2], A_x[2]).then_inc(patch_in[2], 16)
            sp.dma_start(raw[1][:, 0:DK * QKV], A_wqkv).then_inc(wqkv_in, 16)
            sp.dma_start(patches[:, 3], A_x[3]).then_inc(patch_in[3], 16)
            for dst, src in ((rw, A_rw), (gamma, A_gamma.partition_broadcast(P)), (beta, A_beta.partition_broadcast(P)),
                             (rb, A_rb.partition_broadcast(P)), (wo, A_wo), (bdown, A_bdown), (sel, A_sel)):
                sp.dma_start(dst[:], src).then_inc(small_in, 16)
            for t in range(4, NT):
                arrived(sp, ("tok", t - 4))
                sp.dma_start(patches[:, t % 4], A_x[t]).then_inc(patch_in[t % 4], 16)
            arrived(sp, ("tok", NT - 1))
            sp.dma_start(raw[0][:], A_wffn[0]).then_inc(raw_in[0], 16)
            for k in range(DK):
                sp.wait_ge(wql_ready[k], 1)
            sp.wait_ge(scored, TPH)
            sp.dma_start(raw[1][:], A_wffn[1]).then_inc(raw_in[1], 16)
            with sp.Fori(1, EXPERTS // 2) as it:
                for i in range(2):
                    sp.wait_ge(wlo_ready, it * (2 * PIECES) + (i - 1) * PIECES)
                    sp.dma_start(raw[i][:], A_wffn[bass.ds(it * 2 + i, 1)].rearrange("e p n -> (e p) n"))\
                        .then_inc(raw_in[i], 16)
            for t in range(NT):
                sp.wait_ge(out_ready, t + 1)
                sp.dma_start(out[t * P:(t + 1) * P, :], h[:, t]).then_inc(out_done, 16)
            sp.wait_ge(out_done, 16 * NT)

        PER = 2 * 2 * IC
        LAST = EXPERTS // 2 - 1
        FIRST = sum(kind == "step" for kind, _ in order)

        def loop(eng, step, output):
            with eng.Fori(0, LAST) as it:
                for p in range(FIRST, FIRST + PER):
                    step(it, p)
            for p in range(FIRST, PER + IC):
                step(LAST, p)
                if p >= PER:
                    output(p - PER)
            for t in range(IC, NT):
                output(t)

        def no_output(t):
            pass

        def beyond(it, p):
            return isinstance(it, int) and (it == LAST and p >= PER or it == 0 and p < 0)

        def begins(it, p, slots):
            return isinstance(it, int) and it == 0 and p < slots

        def split_piece(it, p):
            k = p % (2 * IC) - 2
            if k < 0 or isinstance(it, int) and it == LAST and p >= 2 * IC:
                return None
            return it * 2 + p // (2 * IC) + 1, (p // (2 * IC) + 1) % 2, k

        @block.tensor
        def _(pe):
            def claim(job):
                for b in place[job]:
                    claim_bank(job, b)

            def claim_bank(job, b):
                if before[job][b]:
                    pe.wait_ge(free[b], before[job][b])

            def split_product(dst, wh, wl, xhi, xlo, first, last):
                nc.tensor.matmul(dst, wh, xhi, start=first, stop=False)
                nc.tensor.matmul(dst, wh, xlo, start=False, stop=False)
                return nc.tensor.matmul(dst, wl, xhi, start=False, stop=last)

            def gate_up(it, p):
                s = p % 2
                e, half, m = (p // (2 * IC)) % 2, (p // IC) % 2, p % IC
                if p % (2 * IC) == 0:
                    n = (it * 2 + p // (2 * IC)) * PIECES + GU_PIECES
                    pe.wait_ge(whi_ready, n)
                    pe.wait_ge(wlo_ready, n)
                for src, ps in ((0, gate_ps), (1, up_ps)):
                    if not begins(it, p, 2):
                        pe.wait_ge((gate_done, up_done)[src], it * PER + p - 1)
                    for c in range(DK):
                        col = c * 2 * INNER + src * INNER + m * P
                        last = split_product(ps[s], whi[e][:, col:col + P], wlo[e][:, col:col + P],
                                             xh[:, c, half * HALF:(half + 1) * HALF],
                                             xl[:, c, half * HALF:(half + 1) * HALF], c == 0, c == DK - 1)
                    last.then_inc(gu_ready, 1)

            def down(it, p):
                e, m, s = (p // (2 * IC)) % 2, p % IC, p % 4
                if p % (2 * IC) == 0:
                    n = (it * 2 + p // (2 * IC) + 1) * PIECES
                    pe.wait_ge(whi_ready, n)
                    pe.wait_ge(wlo_ready, n)
                if begins(it, p, 1):
                    pe.wait_ge(free[0], experts_from[0])
                    pe.wait_ge(free[1], experts_from[1])
                biased = m == 0 and begins(it, p, 2 * IC)
                if biased:
                    taken(pe, ("cTf", p // IC))
                if beyond(it, p + 1):
                    pe.wait_ge(last_al_ready, 1)
                else:
                    pe.wait_ge(al_ready, it * PER + p + 1)
                for c in range(DK):
                    if m == 0 and not begins(it, p, 1):
                        pe.wait_ge(y_added, it * (PER // IC * DK) + (p // IC - 1) * DK + c + 1)
                    if biased:
                        nc.tensor.matmul(y_ps[c][:], bdown[:, c * P:(c + 1) * P], cTf[p // IC], start=True, stop=False)
                    col = GU + m * D + c * P
                    last = split_product(y_ps[c][:], whi[e][:, col:col + P], wlo[e][:, col:col + P],
                                         ah[:, s], al[:, s], m == 0 and not biased, m == IC - 1)
                last.then_inc(down_done, 1)

            def share(it, unit):
                half = unit % 2
                if not begins(it, unit, 2):
                    pe.wait_ge(a_done, it * PER + (unit - 1) * IC)
                expert = sel[:, bass.ds(it * 2 + unit // 2, 1)].rearrange("p e n -> p (e n)")
                nc.tensor.matmul(share_ps[half][:], expert,
                                 cT[:, half * HALF:(half + 1) * HALF], start=True, stop=True).then_inc(share_ready, 1)

            def step(it, p):
                if not beyond(it, p):
                    gate_up(it, p)
                if p % IC == 2 and p > IC and not beyond(it, p + IC):
                    share(it, p // IC + 1)
                if not beyond(it, p - LAG):
                    down(it, p - LAG)

            def output(t):
                if t == 0:
                    pe.wait_ge(gate_done, EXPERTS * 2 * IC)
                    pe.wait_ge(up_done, EXPERTS * 2 * IC)
                    pe.wait_ge(y_added, EXPERTS * 2 * DK - DK)
                if t < TPH:
                    for c in range(DK):
                        last = turned(t, c)
                    last.then_inc(turned_ready, 1)
                if t == TPH:
                    for c in range(DK):
                        pe.wait_ge(y_added, EXPERTS * 2 * DK - DK + c + 1)
                        for u in range(TPH, NT):
                            if c == 0:
                                pe.wait_ge(out_ready, u - TPH + 1)
                            last = turned(u, c)
                            if c == DK - 1:
                                last.then_inc(turned_ready, 1)

            def turned(t, c):
                return nc.tensor.transpose(scores[:, t % TPH, c * P:(c + 1) * P], yacc[:, c, t * P:(t + 1) * P], ident)

            for kind, at in pe_order:
                job = (kind, at)
                if kind in RELEASES and kind != "mix":
                    claim(job)
                if kind == "tok":
                    pe.wait_ge(patch_in[at % 4], 16 * (at // 4 + 1))
                    for k in range(FK):
                        if at == 0 and k % (FK // DK) == 0:
                            pe.wait_ge(wtok_in[k // (FK // DK)], 16)
                        last = nc.tensor.matmul(bank(job)[:, 0:D], patches[:, at % 4, k, :], wtok[:, k // 3, k % 3, :],
                                                start=(k == 0), stop=(k == FK - 1))
                    last.then_inc(ready, 1)
                elif kind in ("x1T", "x2T", "yT"):
                    if kind == "x1T":
                        pe.wait_ge(x1_ready, at + 1)
                        src = x1[:, at]
                        if at == 0:
                            pe.wait_ge(const_in, 16)
                    elif kind == "x2T":
                        pe.wait_ge(x2_ready, at + 1)
                        src = x2[:, at % 2]
                    else:
                        taken(pe, ("mix", at))
                        src = yn[:, at % 2]
                    for c in range(DK):
                        last = nc.tensor.transpose(bank(job)[:, c * P:(c + 1) * P], src[:, c * P:(c + 1) * P], ident)
                    last.then_inc(ready, 1)
                elif kind in ("q", "qs", "k", "ks"):
                    half, c = at
                    if kind == "q" and c == 0:
                        if half == 0:
                            pe.wait_ge(wqh_ready, DK)
                            for k in range(DK):
                                pe.wait_ge(wql_ready[k], 1)
                        for t in range(half * TPH, half * TPH + TPH):
                            taken(pe, ("x1T", t))
                    col = ("q", "qs", "k", "ks").index(kind) * D + c * P
                    for k in range(DK):
                        last = split_product(bank(job)[:], wqh[:, k, col:col + P], wql[:, k, col:col + P],
                                             xh[:, k, half * HALF:(half + 1) * HALF],
                                             xl[:, k, half * HALF:(half + 1) * HALF], k == 0, k == DK - 1)
                    last.then_inc(ready, 1)
                elif kind == "v":
                    for k in range(DK):
                        a_h, a_l = xh[:, k, at * P:(at + 1) * P], xl[:, k, at * P:(at + 1) * P]
                        last = split_product(bank(job)[:, 0:D], a_h, a_l, wqh[:, k, 4 * D:5 * D],
                                             wql[:, k, 4 * D:5 * D], k == 0, k == DK - 1)
                    last.then_inc(ready, 1)
                elif kind == "scores":
                    half, i0 = at // TPH, at % TPH * P
                    if at % TPH == 0:
                        for c in range(DK):
                            taken(pe, ("q", (half, c)))
                            taken(pe, ("k", (half, c)))
                        pe.wait_ge(roped, 4 * (half + 1))
                    if at >= 1:
                        pe.wait_ge(exped, at)
                    left, right = (kr, qn[half]), (qz[half], kz[half])
                    for kind_col, l, r in zip((0, 128), left, right):
                        for c in range(DK):
                            for j in range(4):
                                for i in range(4):
                                    rows = slice(32 * i, 32 * i + 32)
                                    cols = slice(i0 + 32 * j, i0 + 32 * j + 32)
                                    col = kind_col + c * 64
                                    last = nc.tensor.matmul(scores[32 * j:32 * j + 32, i, col:col + 64],
                                                            l[rows, c, cols], r[rows, c, :, cols],
                                                            start=True, stop=True)
                    last.then_inc(scored, 1)
                elif kind == "mix":
                    pe.wait_ge(p_ready, at + 1)
                    taken(pe, ("v", at))
                    for two in (place[job][0:2], place[job][2:4]):
                        for j in two:
                            claim_bank(job, j)
                        for i in range(4):
                            for cs in range(4):
                                head = (cs // 2) * 8 + i * 2 + cs % 2
                                col = (i * 4 + cs) * DH
                                for j in two:
                                    rows = slice(32 * j, 32 * j + 32)
                                    last = nc.tensor.matmul(banks[j][rows, col:col + DH],
                                                            p_sb[rows, at % 2, i, cs * 32:cs * 32 + 32],
                                                            v[rows, at % TPH, head * DH:(head + 1) * DH],
                                                            start=True, stop=True)
                        last.then_inc(mixed, 1)
                elif kind == "proj":
                    if at == 0:
                        pe.wait_ge(small_in, 16 * 7)
                    taken(pe, ("yT", at))
                    for c in range(DK):
                        last = nc.tensor.matmul(bank(job)[:, 0:D], yt[:, at % 2, c, :], wo[:, c, :],
                                                start=(c == 0), stop=(c == DK - 1))
                    last.then_inc(ready, 1)
                elif kind == "logits":
                    if at == 0:
                        pe.wait_ge(rwh_ready, 1)
                        pe.wait_ge(rwl_ready, 1)
                    for t in range(at * TPH, at * TPH + TPH):
                        taken(pe, ("x2T", t))
                    for k in range(DK):
                        cols = slice(at * HALF, (at + 1) * HALF)
                        last = split_product(bank(job)[:], rwh[:, k], rwl[:, k], xh[:, k, cols], xl[:, k, cols],
                                             k == 0, k == DK - 1)
                    last.then_inc(ready, 1)
                elif kind == "lgT":
                    taken(pe, ("logits", at))
                    for i in range(TPH):
                        last = nc.tensor.transpose(bank(job)[:, i * EXPERTS:(i + 1) * EXPERTS],
                                                   lgT[at][:, i * P:(i + 1) * P], ident[0:EXPERTS, 0:EXPERTS])
                    last.then_inc(ready, 1)
                elif kind == "cT":
                    pe.wait_ge(parts_ready, at + 1)
                    if at == 0:
                        pe.wait_ge(identb_ready, 1)
                    for i in range(TPH):
                        last = nc.tensor.transpose(bank(job)[:].bitcast(BF16)[0:3 * EXPERTS, i * P:(i + 1) * P],
                                                   parts[:, at * TPH + i].rearrange("p a b -> p (a b)"), identb[:])
                    last.then_inc(ready, 1)
                elif kind == "cTf":
                    pe.wait_ge(comb_ready, at + 1)
                    for i in range(TPH):
                        last = nc.tensor.transpose(bank(job)[0:EXPERTS, i * P:(i + 1) * P],
                                                   comb[:, at * TPH + i], ident)
                    last.then_inc(ready, 1)
                elif kind == "share1":
                    taken(pe, ("cT", 1))
                    pe.wait_ge(free[3], experts_from[3])
                    share(0, 1)
                elif kind == "step":
                    if at == 0:
                        pe.wait_ge(exped, NT)
                    if at == IC:
                        for t in range(TPH, NT):
                            taken(pe, ("x2T", t))
                    step(0, at)
                    if at == 0:
                        taken(pe, ("cT", 0))
                        pe.wait_ge(cz_ready, 1)
                        pe.wait_ge(free[2], experts_from[2])
                        share(0, 0)
            loop(pe, step, output)

        @block.scalar
        def _(act_eng):
            def split_high(slot, k):
                nc.scalar.copy(whi[slot][:, k * PIECE:(k + 1) * PIECE],
                               raw[slot][:, k * PIECE:(k + 1) * PIECE]).then_inc(whi_ready, 1)

            def step(it, p):
                n, s = it * PER + p, p % 2
                if not beyond(it, p):
                    act_eng.wait_ge(gate_done, n + 1)
                    if not begins(it, p, 2):
                        act_eng.wait_ge(s_done, n - 1)
                    nc.scalar.activation(tanh[:, s], gate[:, s], ACT.Tanh, scale=ALPHA / 2).then_inc(tanh_done, 1)
                if not beyond(it, p - 1):
                    act_eng.wait_ge(a_done, n)
                    if not begins(it, p - 1, 4):
                        act_eng.wait_ge(down_done, n - 4)
                    nc.scalar.copy(ah[:, (p - 1) % 4], act[:, 1 - s]).then_inc(ah_ready, 1)
                piece = split_piece(it, p)
                if piece:
                    expert, slot, k = piece
                    if k == 0:
                        act_eng.wait_ge(raw_in[slot], (it + (p // (2 * IC) + 1) // 2) * 16 + 16)
                        if not begins(it, p, 2 * IC):
                            act_eng.wait_ge(gu_ready, (expert - 1) * (2 * IC * 2))
                    if k == GU_PIECES and not begins(it, p, 2 * IC):
                        act_eng.wait_ge(down_done, (expert - 1) * (2 * IC))
                    split_high(slot, k)

            for kind, at in order:
                job = (kind, at)
                if kind == "wsplit":
                    if at == 0:
                        act_eng.wait_ge(wqkv_in, 16)
                    nc.scalar.copy(wqh[:, at], raw[1][:, at * QKV:(at + 1) * QKV]).then_inc(wqh_ready, 1)
                elif kind in ("x1T", "x2T"):
                    arrived(act_eng, job)
                    nc.scalar.copy(xh[:, :, at * P:(at + 1) * P],
                                   bank(job)[:, 0:D].rearrange("p (c n) -> p c n", c=DK))\
                        .then_inc(xhi_ready if kind == "x1T" else x2hi_ready, 1)
                elif kind == "q":
                    half, c = at
                    arrived(act_eng, job)
                    nc.scalar.copy(qn[half][:, c], bank(job)[:]).then_inc(freed(job), 1)
                elif kind == "k":
                    half, c = at
                    arrived(act_eng, job)
                    if c == 0 and half == 0:
                        act_eng.wait_ge(const_in, 16)
                    nc.scalar.activation(kz[half][:, c, 0], bank(job)[:], ACT.Copy, scale=even)
                    nc.scalar.activation(kz[half][:, c, 1], bank(job)[:], ACT.Copy, scale=odd)\
                        .then_inc(freed(job), 1)
                elif kind == "v":
                    arrived(act_eng, job)
                    if at == TPH:
                        act_eng.wait_ge(mixed, 2 * TPH)
                    nc.scalar.copy(v[:, at % TPH], bank(job)[:, 0:D]).then_inc(freed(job), 1)
                elif kind == "scores":
                    act_eng.wait_ge(scored, at + 1)
                    if at >= 2:
                        act_eng.wait_ge(p_ready, at - 1)
                        act_eng.wait_ge(den_ready, at - 1)
                    nc.scalar.activation(e_sb[:, at % 2], scores[:, :, 0:256].rearrange("p i (y n) -> p i y n", y=2),
                                         ACT.Exp, scale=SCALE).then_inc(exped, 1)
                elif kind == "yT":
                    arrived(act_eng, job)
                    if at >= 2:
                        arrived(act_eng, ("proj", at - 2))
                    nc.scalar.copy(yt[:, at % 2], bank(job)[:, 0:D].rearrange("p (c n) -> p c n", c=DK))\
                        .then_inc(freed(job), 1)
                elif kind == "split":
                    if at == 0:
                        act_eng.wait_ge(const_in, 16)
                        nc.scalar.copy(identb[:], ident).then_inc(identb_ready, 1)
                        act_eng.wait_ge(small_in, 16 * 7)
                        nc.scalar.copy(rwh[:], rw[:]).then_inc(rwh_ready, 1)
                        act_eng.wait_ge(raw_in[0], 16)
                    split_high(0, at)
                elif kind == "logits":
                    arrived(act_eng, job)
                    nc.scalar.copy(lgT[at], bank(job)[0:EXPERTS, :]).then_inc(freed(job), 1)
                elif kind == "router":
                    act_eng.wait_ge(lsub_ready, at + 1)
                    tiles = slice(at * TPH, (at + 1) * TPH)
                    nc.scalar.activation(ex[:, tiles], ex[:, tiles], ACT.Exp).then_inc(ex_ready, 1)
                elif kind == "cTf":
                    arrived(act_eng, job)
                    nc.scalar.copy(cTf[at], bank(job)[0:EXPERTS, :]).then_inc(freed(job), 1)
                elif kind == "cT":
                    arrived(act_eng, job)
                    act_eng.wait_ge(cz_ready, 1)
                    nc.scalar.copy(cT[0:3 * EXPERTS, at * HALF:(at + 1) * HALF],
                                   bank(job)[:].bitcast(BF16)[0:3 * EXPERTS, 0:HALF]).then_inc(freed(job), 1)
                elif kind == "step":
                    step(0, at)
            loop(act_eng, step, no_output)

        @block.gpsimd
        def _(pool):
            links = [0]

            def link(ins):
                links[0] += 1
                ins.then_inc(pchain, 1)
                pool.wait_ge(pchain, links[0])

            def split_low(slot, k):
                cols = slice(k * PIECE, (k + 1) * PIECE)
                nc.gpsimd.tensor_tensor(wlo[slot][:, cols], raw[slot][:, cols], whi[slot][:, cols].bitcast(F32),
                                        ALU.subtract).then_inc(wlo_ready, 1)

            def split_bias(slot):
                nc.gpsimd.tensor_tensor(bias[slot][:], raw[slot][:, WCOLS:WROW], offset[:], ALU.add)\
                    .then_inc(bias_ready, 1)

            def root(i, t):
                pool.wait_ge(var_ready[i], t + 1)
                nc.gpsimd.tensor_tensor(rstd[:, i, t], ve[:, i, t], power[:], ALU.pow).then_inc(rstd_ready[i], 1)

            def step(it, p):
                n = it * PER + p
                piece = split_piece(it, p)
                if piece:
                    expert, slot, k = piece
                    pool.wait_ge(whi_ready, expert * PIECES + k + 1)
                    if k == 0:
                        if not begins(it, p, 2 * IC):
                            pool.wait_ge(up_done, (expert - 1) * (2 * IC))
                        split_bias(slot)
                    split_low(slot, k)
                if not beyond(it, p - 1) and not beyond(it, p):
                    pool.wait_ge(ah_ready, n)
                    nc.gpsimd.tensor_tensor(al[:, (p - 1) % 4], act[:, (p - 1) % 2], ah[:, (p - 1) % 4].bitcast(F32),
                                            ALU.subtract).then_inc(al_ready, 1)

            nc.gpsimd.memset(power[:], -0.5)
            nc.gpsimd.memset(offset[:, 0:IC], 0.0)
            link(nc.gpsimd.memset(offset[:, IC:2 * IC], 1.0))
            nc.gpsimd.memset(cT[:], 0.0).then_inc(cz_ready, 1)
            for kind, at in order:
                if kind == "tok":
                    root(0, at)
                elif kind == "wsplit" and at == 0:
                    pool.wait_ge(wqh_ready, at + 1)
                    nc.gpsimd.tensor_tensor(wql[:, at], raw[1][:, at * QKV:(at + 1) * QKV], wqh[:, at].bitcast(F32),
                                            ALU.subtract).then_inc(wql_ready[at], 1)
                elif kind in ("qs", "ks"):
                    half, c = at
                    taken(pool, (kind[0], at))
                    taken(pool, (kind, at))
                    b = "qk".index(kind[0])
                    if half and kind == "ks" and c == 0:
                        pool.wait_ge(scored, TPH)
                    if kind == "qs":
                        link(nc.gpsimd.tensor_tensor(ropec[:, b], ropec[:, b], ropes[:, b], ALU.add))
                        nc.gpsimd.tensor_scalar(qz[half][:, c, 0], ropec[:, b], even, 1.0, ALU.mult, ALU.mult)
                        nc.gpsimd.tensor_scalar(qz[half][:, c, 1], ropec[:, b], odd, 1.0, ALU.mult, ALU.mult)\
                            .then_inc(roped, 1)
                    else:
                        nc.gpsimd.tensor_tensor(kr[:, c], ropec[:, b], ropes[:, b], ALU.add).then_inc(roped, 1)
                elif kind == "mask":
                    pool.wait_ge(exped, at + 1)
                    if at == 0:
                        pool.wait_ge(const_in, 16)
                    plain = e_sb[:, at % 2, :, 1].rearrange("p i (g n) -> p i g n", n=32)
                    same = const[:, C_MASK:C_MASK + 32].unsqueeze(1).unsqueeze(1).broadcast_to([P, 4, 4, 32])
                    nc.gpsimd.tensor_tensor(plain, plain, same, ALU.mult).then_inc(plain_ready, 1)
                elif kind == "proj":
                    root(1, at)
                elif kind == "norm2":
                    pool.wait_ge(zn_ready, at + 1)
                    link(nc.gpsimd.tensor_tensor(z[:, at % 2], z[:, at % 2], gamma[:], ALU.mult))
                    link(nc.gpsimd.tensor_tensor(z[:, at % 2], z[:, at % 2], beta[:], ALU.add))
                    nc.gpsimd.tensor_tensor(h[:, at], h[:, at], z[:, at % 2], ALU.add).then_inc(h1_ready, 1)
                elif kind == "spread3":
                    root(2, at)
                elif kind == "split":
                    if at == 0:
                        pool.wait_ge(rwh_ready, 1)
                        nc.gpsimd.tensor_tensor(rwl[:], rw[:], rwh[:].bitcast(F32), ALU.subtract)\
                            .then_inc(rwl_ready, 1)
                        pool.wait_ge(raw_in[0], 16)
                        split_bias(0)
                    pool.wait_ge(whi_ready, at + 1)
                    split_low(0, at)
                elif kind == "step":
                    if at == 0:
                        pool.wait_ge(scored, NT)
                        nc.gpsimd.memset(yacc[:], 0.0).then_inc(zeroed, 1)
                    step(0, at)
            loop(pool, step, no_output)

        @block.vector
        def _(dve):
            links = [0]

            def link(ins):
                links[0] += 1
                ins.then_inc(chain, 1)
                dve.wait_ge(chain, links[0])

            def spread(i, t, src):
                link(nc.vector.bn_stats(stat[:, i, t], src))
                link(nc.vector.bn_aggr(mv[:, i, t], stat[:, i, t]))
                nc.vector.tensor_scalar(ve[:, i, t], mv[:, i, t, 1:2], EPS, None, ALU.add).then_inc(var_ready[i], 1)

            def normal(i, t, dst, src):
                dve.wait_ge(rstd_ready[i], t + 1)
                return nc.vector.tensor_scalar(dst, src, mv[:, i, t, 0:1], rstd[:, i, t], ALU.subtract, ALU.mult)

            def table(col):
                return const[:, col:col + SEQ].unsqueeze(1).broadcast_to([P, HALF // SEQ, SEQ])

            def route(at):
                tiles = slice(at * TPH, (at + 1) * TPH)
                l, x, c, r, m = lg[:, tiles], ex[:, tiles], comb[:, tiles], rest[:, tiles], lmax[:, tiles]
                k = rank[:, tiles]
                taken(dve, ("lgT", at))
                link(nc.vector.tensor_reduce(m, l, AX, ALU.max))
                nc.vector.tensor_tensor(x, l, m.unsqueeze(2).broadcast_to([P, TPH, EXPERTS]),
                                        ALU.subtract).then_inc(lsub_ready, 1)
                grid = [P, TPH, EXPERTS, EXPERTS]
                other, own = l.unsqueeze(2).broadcast_to(grid), l.unsqueeze(3).broadcast_to(grid)
                by_pair = above[:].rearrange("p (t a b) -> p t a b", t=TPH, a=EXPERTS)
                nc.vector.tensor_tensor(by_pair, other, own, ALU.is_gt)
                link(nc.vector.tensor_tensor(equal[:].rearrange("p (t a b) -> p t a b", t=TPH, a=EXPERTS), other, own,
                                             ALU.is_equal))
                before = const[:, C_TRI:C_COLS].unsqueeze(1).broadcast_to([P, TPH, EXPERTS * EXPERTS])
                flat = equal[:].rearrange("p (t n) -> p t n", t=TPH)
                link(nc.vector.tensor_tensor(flat, flat, before, ALU.mult))
                link(nc.vector.tensor_tensor(above[:], above[:], equal[:], ALU.add))
                link(nc.vector.tensor_reduce(k, by_pair, AX, ALU.add))
                link(nc.vector.tensor_scalar(k, k, TOPK - 0.5, None, ALU.is_lt))
                dve.wait_ge(ex_ready, at + 1)
                link(nc.vector.tensor_tensor(c, x, k, ALU.mult))
                link(nc.vector.tensor_reduce(m, c, AX, ALU.add))
                link(nc.vector.reciprocal(m, m))
                nc.vector.tensor_tensor(c, c, m.unsqueeze(2).broadcast_to([P, TPH, EXPERTS]), ALU.mult)\
                    .then_inc(comb_ready, 1)
                dve.wait_ge(comb_ready, at + 1)
                link(nc.vector.tensor_copy(parts[:, tiles, 0], c))
                link(nc.vector.tensor_tensor(r, c, parts[:, tiles, 0], ALU.subtract))
                link(nc.vector.tensor_copy(parts[:, tiles, 1], r))
                link(nc.vector.tensor_tensor(r, r, parts[:, tiles, 1], ALU.subtract))
                nc.vector.tensor_copy(parts[:, tiles, 2], r).then_inc(parts_ready, 1)

            def add_up(it, unit):
                half = unit % 2
                n = it * (PER // IC) + unit
                dve.wait_ge(down_done, n * IC + IC)
                if begins(it, unit, 1):
                    dve.wait_ge(zeroed, 1)
                else:
                    dve.wait_ge(y_added, n * DK)
                for c in range(DK):
                    dst = yacc[:, c, half * HALF:(half + 1) * HALF]
                    nc.vector.tensor_tensor(dst, y_ps[c][:], dst, ALU.add).then_inc(y_added, 1)

            def step(it, p):
                n, s, f = it * PER + p, p % 2, (p - 1) % 2
                if p % IC == LAG and not beyond(it, p - IC):
                    add_up(it, p // IC - 1)
                now, then = not beyond(it, p), not beyond(it, p - 1)
                b, m = bias[(p // (2 * IC)) % 2], p % IC
                if now:
                    if p % (2 * IC) == 0:
                        dve.wait_ge(bias_ready, it * 2 + p // (2 * IC) + 1)
                    dve.wait_ge(gu_ready, n * 2 + 1)
                    nc.vector.tensor_scalar(gate[:, s], gate_ps[s], b[:, m:m + 1], LIMIT, ALU.add, ALU.min)\
                        .then_inc(gate_done, 1)
                if then:
                    dve.wait_ge(s_done, n)
                    nc.vector.scalar_tensor_tensor(out=up[:, f], in0=up[:, f], scalar=1.0 - LIMIT, in1=gate[:, f],
                                                   op0=ALU.max, op1=ALU.mult).then_inc(m_done, 1)
                if now:
                    dve.wait_ge(gu_ready, n * 2 + 2)
                    if not begins(it, p, 2):
                        dve.wait_ge(a_done, n - 1)
                    nc.vector.tensor_scalar(up[:, s], up_ps[s], b[:, IC + m:IC + m + 1], LIMIT + 1, ALU.add,
                                            ALU.min).then_inc(up_done, 1)
                if then:
                    dve.wait_ge(m_done, n)
                    if not begins(it, p - 1, 2):
                        dve.wait_ge(al_ready, n - 2)
                    unit = (p - 1) // IC
                    dve.wait_ge(share_ready, it * (PER // IC) + unit + 1)
                    nc.vector.tensor_tensor(act[:, f], up[:, f], share_ps[unit % 2][:], ALU.mult).then_inc(a_done, 1)
                if then and not now and it == LAST:
                    dve.wait_ge(ah_ready, n)
                    nc.vector.tensor_tensor(al[:, (p - 1) % 4], act[:, f], ah[:, (p - 1) % 4].bitcast(F32),
                                            ALU.subtract).then_inc(last_al_ready, 1)
                if now:
                    dve.wait_ge(tanh_done, n + 1)
                    nc.vector.scalar_tensor_tensor(out=gate[:, s], in0=tanh[:, s], scalar=1.0, in1=gate[:, s],
                                                   op0=ALU.add, op1=ALU.mult).then_inc(s_done, 1)

            def output(t):
                dve.wait_ge(turned_ready, t + 1)
                nc.vector.tensor_tensor(h[:, t], scores[:, t % TPH, 0:D], h[:, t], ALU.add).then_inc(out_ready, 1)

            dve.wait_ge(rows_in, 16 * 2)
            link(nc.vector.tensor_tensor(pos[:], pos[:], tokb[:], ALU.add))
            for kind, at in order:
                job = (kind, at)
                if kind == "tok":
                    arrived(dve, job)
                    nc.vector.tensor_tensor(h[:, at], bank(job)[:, 0:D], pos[:], ALU.add).then_inc(freed(job), 1)
                    taken(dve, job)
                    spread(0, at, h[:, at])
                elif kind == "norm1":
                    normal(0, at, x1[:, at], h[:, at]).then_inc(x1_ready, 1)
                elif kind == "wsplit" and at == 1:
                    dve.wait_ge(wqh_ready, at + 1)
                    nc.vector.tensor_tensor(wql[:, at], raw[1][:, at * QKV:(at + 1) * QKV], wqh[:, at].bitcast(F32),
                                            ALU.subtract).then_inc(wql_ready[at], 1)
                elif kind in ("x1T", "x2T"):
                    dve.wait_ge(xhi_ready if kind == "x1T" else x2hi_ready, at + 1)
                    cols = slice(at * P, (at + 1) * P)
                    nc.vector.tensor_tensor(xl[:, :, cols], bank(job)[:, 0:D].rearrange("p (c n) -> p c n", c=DK),
                                            xh[:, :, cols].bitcast(F32), ALU.subtract).then_inc(freed(job), 1)
                elif kind in ("q", "qs", "k", "ks"):
                    half, c = at
                    if kind == "q" and half == 0 and c == 0:
                        dve.wait_ge(const_in, 16)
                    arrived(dve, job)
                    if kind in "qk":
                        dve.wait_ge(freed(job), through[job][place[job][0]] - 1)
                    earlier = [n for n, s in enumerate(sums[0:sums.index((kind[0] + "s", at))]) if s[0][0] == kind[0]]
                    if earlier:
                        dve.wait_ge(roped, earlier[-1] + 1)
                    dst = (ropes if kind[1:] else ropec)[:, "qk".index(kind[0])]
                    nc.vector.tensor_tensor(dst.rearrange("p (b s) -> p b s", s=SEQ),
                                            bank(job)[:].rearrange("p (b s) -> p b s", s=SEQ),
                                            table(C_SIN if kind[1:] else C_COS), ALU.mult).then_inc(freed(job), 1)
                elif kind == "mask":
                    b = at % 2
                    if at >= 2:
                        dve.wait_ge(mixed, 2 * (at - 1))
                    dve.wait_ge(exped, at + 1)
                    same = const[:, C_MASK:C_MASK + 32].unsqueeze(1).unsqueeze(1).broadcast_to([P, 4, 4, 32])
                    nc.vector.tensor_tensor(p_sb[:, b].rearrange("p i (g n) -> p i g n", n=32),
                                            e_sb[:, b, :, 0].rearrange("p i (g n) -> p i g n", n=32),
                                            same, ALU.mult).then_inc(p_ready, 1)
                elif kind == "den":
                    b = at % 2
                    dve.wait_ge(plain_ready, at + 1)
                    plain = e_sb[:, b, :, 1].rearrange("p i (g n) -> p i g n", n=32)
                    nc.vector.tensor_reduce(den[:, b].rearrange("p (i g) -> p i g", g=4), plain, AX, ALU.add)\
                        .then_inc(den_ready, 1)
                    dve.wait_ge(den_ready, at + 1)
                    link(nc.vector.reciprocal(rden[:, b], den[:, b]))
                elif kind == "mix":
                    b = at % 2
                    if at >= 2:
                        arrived(dve, ("yT", at - 2))
                    for n, j in enumerate(place[job]):
                        dve.wait_ge(mixed, 2 * at + n // 2 + 1)
                        rows = slice(32 * j, 32 * j + 32)
                        nc.vector.tensor_tensor(yn[rows, b].rearrange("p (g n) -> p g n", n=DH),
                                                banks[j][rows, 0:D].rearrange("p (g n) -> p g n", n=DH),
                                                rden[rows, b].unsqueeze(2).broadcast_to([32, HEADS, DH]),
                                                ALU.mult).then_inc(free[j], 1)
                elif kind == "proj":
                    arrived(dve, job)
                    if at >= 2:
                        dve.wait_ge(h1_ready, at - 1)
                    nc.vector.tensor_tensor(z[:, at % 2], bank(job)[:, 0:D], x1[:, at], ALU.add)\
                        .then_inc(freed(job), 1)
                    taken(dve, job)
                    spread(1, at, z[:, at % 2])
                elif kind == "norm2":
                    normal(1, at, z[:, at % 2], z[:, at % 2]).then_inc(zn_ready, 1)
                elif kind == "spread3":
                    dve.wait_ge(h1_ready, at + 1)
                    spread(2, at, h[:, at])
                elif kind == "norm3":
                    if at >= 2:
                        arrived(dve, ("x2T", at - 2))
                    normal(2, at, x2[:, at % 2], h[:, at]).then_inc(x2_ready, 1)
                elif kind == "lgT":
                    if at == 0:
                        dve.wait_ge(small_in, 16 * 7)
                    arrived(dve, job)
                    nc.vector.tensor_tensor(lg[:, at * TPH:(at + 1) * TPH],
                                            bank(job)[:, 0:TPH * EXPERTS].rearrange("p (t e) -> p t e", t=TPH),
                                            rb[:].unsqueeze(1).broadcast_to([P, TPH, EXPERTS]), ALU.add)\
                        .then_inc(freed(job), 1)
                elif kind == "router":
                    route(at)
                elif kind == "step":
                    if at == 0:
                        dve.wait_ge(roped, 4 * 2)
                    step(0, at)
            loop(dve, step, output)


def constants():
    c = np.zeros((P, C_COLS), np.float32)
    c[:, C_ID:C_ID + P] = np.eye(P)
    p = np.arange(P)
    c[:, C_MASK:C_MASK + 32] = (p[:, None] % 32) // SEQ == np.arange(32)[None, :] // SEQ
    c[:, C_EVEN] = p // DH % 2 == 0
    c[:, C_ODD] = p // DH % 2 == 1
    i = np.arange(1, DH // 2 + 1, dtype=np.float32)
    theta = np.repeat(np.float32(1000.0) ** (np.float32(-2.0) * i / np.float32(DH)), 2)
    args = np.arange(1, SEQ + 1, dtype=np.float32)[:, None] * theta[None, :]
    sign = np.where(np.arange(DH) % 2 == 0, -1, 1).astype(np.float32)
    c[:, C_COS:C_COS + SEQ] = np.tile(np.cos(args).T, (P // DH, 1))
    c[:, C_SIN:C_SIN + SEQ] = np.tile((np.sin(args) * sign).T, (P // DH, 1))
    e = np.arange(EXPERTS)
    c[:, C_TRI:] = (e[None, :] < e[:, None]).reshape(1, -1)
    return c


def kernel(x, L0_tok_W, L0_tok_b, L0_tok_pos_emb, L0_attn_w_in, L0_attn_w_out, L0_attn_ln_gamma, L0_attn_ln_beta,
           L0_ffn_router_weight, L0_ffn_router_bias, L0_ffn_gate_up_proj, L0_ffn_gate_up_proj_bias, L0_ffn_down_proj,
           L0_ffn_down_proj_bias):
    import ml_dtypes
    import concourse.bacc as bacc
    from concourse.bass_utils import run_bass_kernel_spmd

    def rows(w, chunks):
        return w.reshape(chunks, P, -1).transpose(1, 0, 2)

    x = np.asarray(x).reshape(IMAGES, CH, GRID, PS, GRID, PS).transpose(1, 3, 5, 0, 2, 4).reshape(FK, P, NT, P)
    x = x.transpose(2, 1, 0, 3).reshape(NT, P, FK * P)
    w_in = np.asarray(L0_attn_w_in)
    swap = np.arange(D) ^ 1
    q, k, v = w_in[0:D], w_in[D:2 * D], w_in[2 * D:]
    wqkv = rows(np.concatenate([q, q[swap], k, k[swap], v]).T, DK).reshape(P, DK * QKV)
    heads = np.arange(HEADS).reshape(DK, 4, 2).transpose(1, 0, 2).ravel()
    wo = np.asarray(L0_attn_w_out).T.reshape(HEADS, DH, D)[heads].reshape(D, D)
    gu = np.asarray(L0_ffn_gate_up_proj).transpose(0, 2, 1).reshape(EXPERTS, DK, P, 2 * INNER).transpose(0, 2, 1, 3)
    down = np.asarray(L0_ffn_down_proj).transpose(0, 2, 1).reshape(EXPERTS, IC, P, D).transpose(0, 2, 1, 3)
    gub = np.asarray(L0_ffn_gate_up_proj_bias).reshape(EXPERTS, 2 * IC, P).transpose(0, 2, 1)
    wffn = np.concatenate([gu.reshape(EXPERTS, P, -1), down.reshape(EXPERTS, P, -1), gub], axis=2)
    sel = np.zeros((P, EXPERTS, P), np.float32)
    for part in range(3):
        for e in range(EXPERTS):
            sel[part * EXPERTS + e, e] = 0.5
    rw = np.zeros((P, DK, P), np.float32)
    rw[:, :, 0:EXPERTS] = rows(np.asarray(L0_ffn_router_weight).T, DK)
    arrays = {
        "x": x, "wtok": rows(np.asarray(L0_tok_W).T, FK), "tokb": np.asarray(L0_tok_b),
        "pos": np.tile(np.asarray(L0_tok_pos_emb), (P // SEQ, 1)), "wqkv": wqkv, "wo": rows(wo, DK),
        "gamma": np.asarray(L0_attn_ln_gamma),
        "beta": np.asarray(L0_attn_ln_beta), "rw": rw,
        "rb": np.asarray(L0_ffn_router_bias), "wffn": wffn, "bdown": np.asarray(L0_ffn_down_proj_bias),
        "const": constants(), "sel": sel.astype(ml_dtypes.bfloat16),
    }
    arrays = {n: np.ascontiguousarray(a) for n, a in arrays.items()}
    nc = bacc.Bacc("TRN2", target_bir_lowering=False, num_devices=1)
    args = [nc.dram_tensor(f"in_{n}", a.shape, mybir.dt.from_np(a.dtype), kind="ExternalInput").ap()
            for n, a in arrays.items()]
    out = nc.dram_tensor("out", [TOK, D], F32, kind="ExternalOutput").ap()
    build(nc, *args, out)
    r = run_bass_kernel_spmd(nc, [{f"in_{n}": a for n, a in arrays.items()}], core_ids=[0])
    return r.results[0]["out"].reshape(IMAGES, SEQ, D)
```
